# Optimizing a Trainium2 kernel written in Bass

```python
import numpy as np
import jax
import jax.numpy as jnp

def _softmax(x, axis=-1):
    return jax.nn.softmax(x, axis=axis)

def _gelu(x):
    return jax.nn.gelu(x, approximate=True)

def _silu(x):
    return jax.nn.silu(x)

def _sigmoid(x):
    return jax.nn.sigmoid(x)

def _layernorm(x, axis=-1, eps=1e-05):
    m = jnp.mean(x, axis=axis, keepdims=True)
    v = jnp.var(x, axis=axis, keepdims=True)
    return (x - m) / jnp.sqrt(v + eps)

def _scatter_add(tgt, idx, src, axis=0):
    return tgt.at[idx].add(src)

def _segment_sum(src, seg, n):
    return jax.ops.segment_sum(src, seg, n)
kernel_name = 'mk_xattn_ffn_d2_seqx_r8_3eaf5f'

def setup_inputs(seed: int=0):
    np.random.seed(seed)
    _w = jnp.asarray

    def _rec_inputs():
        import jax
        import jax.numpy as jnp
        _rk = jax.random.key(seed)
        x = -0.0002928 + 1 * jax.random.normal(jax.random.fold_in(_rk, 1), (32, 56, 128), jnp.float32)
        _lenS = 56 - jax.random.randint(jax.random.fold_in(_rk, 7), (32,), 0, max(1, 56 // 4) + 1, jnp.int32)
        _lenS2 = 1500 - jax.random.randint(jax.random.fold_in(_rk, 8), (32,), 0, max(1, 1500 // 4) + 1, jnp.int32)
        _ctx_1024P = jax.random.normal(jax.random.fold_in(_rk, 11), (32, 16, 128), jnp.float32)
        _ctx_1024c = jax.random.dirichlet(jax.random.fold_in(_rk, 511), 0.3 * jnp.ones((16,), jnp.float32), (32, 1500))
        _ctx_1024t = jnp.einsum('bsk,bkd->bsd', _ctx_1024c, _ctx_1024P)
        _ctx_1024t = _ctx_1024t * jax.lax.rsqrt(jnp.mean(jnp.square(_ctx_1024t)) + 1e-12) * 0.953939
        ctx_1024 = -1.39393e-06 + 0.999914 * (_ctx_1024t + 0.3 * jax.random.normal(jax.random.fold_in(_rk, 611), (32, 1500, 128), jnp.float32))
        _validS = jnp.arange(56)[None, :] < _lenS[:, None]
        _validS2 = jnp.arange(1500)[None, :] < _lenS2[:, None]
        _causal = jnp.tril(jnp.ones((56, 56), dtype=bool))
        mask_1x1xSxS2_ik0 = jnp.where(jnp.broadcast_to(_validS2[0:1, None, None, :], (1, 1, 56, 1500)), 0, 1).astype(jnp.int32)
        mask_1x1xSxS2_bk0 = jnp.logical_not(jnp.broadcast_to(_validS2[0:1, None, None, :], (1, 1, 56, 1500)))
        return (x, ctx_1024, mask_1x1xSxS2_ik0, mask_1x1xSxS2_bk0)
    x, ctx_1024, mask_1x1xSxS2_ik0, mask_1x1xSxS2_bk0 = _rec_inputs()

    def _L0_xattn_setup():
        import jax, jax.numpy as jnp
        import numpy as np
        D_MODEL = 128
        NUM_HEADS = 16
        HEAD_DIM = D_MODEL // NUM_HEADS
        B, S = (2, 256)
        key = jax.random.key(seed)
        ks = jax.random.split(key, 12)
        sc = 1.0 / np.sqrt(D_MODEL)
        inp = {'query': jax.random.normal(ks[0], (B, S, D_MODEL), jnp.float32), 'key': jax.random.normal(ks[1], (B, S, D_MODEL), jnp.float32), 'value': jax.random.normal(ks[2], (B, S, D_MODEL), jnp.float32), 'mask': jnp.tril(jnp.ones((S, S), jnp.int32))[None, None, :, :], 'Wq': jax.random.normal(ks[3], (D_MODEL, D_MODEL), jnp.float32) * sc, 'bq': jax.random.normal(ks[4], (D_MODEL,), jnp.float32) * 0.02, 'Wk': jax.random.normal(ks[5], (D_MODEL, D_MODEL), jnp.float32) * sc, 'bk': jax.random.normal(ks[6], (D_MODEL,), jnp.float32) * 0.02, 'Wv': jax.random.normal(ks[7], (D_MODEL, D_MODEL), jnp.float32) * sc, 'bv': jax.random.normal(ks[8], (D_MODEL,), jnp.float32) * 0.02, 'Wo': jax.random.normal(ks[9], (D_MODEL, D_MODEL), jnp.float32) * sc, 'bo': jax.random.normal(ks[10], (D_MODEL,), jnp.float32) * 0.02}
        return inp
    _L0_xattn_all = _L0_xattn_setup()
    _L0_xattn_in = {k: v for k, v in _L0_xattn_all.items() if k in ('Wq', 'bq', 'Wk', 'bk', 'Wv', 'bv', 'Wo', 'bo')}
    del _L0_xattn_all

    def _L0_ffn_setup():
        import jax, jax.numpy as jnp
        import numpy as np
        D = 128
        I = 64
        E = 32
        K = 4
        T = 2 * 256
        C = 2 * T * K // E
        key = jax.random.key(seed)
        ks = jax.random.split(key, 9)
        bf = jnp.bfloat16
        std = 0.02
        x = jax.random.normal(ks[0], (2, 256, D), dtype=jnp.float32).astype(bf)
        gate_w = (std * jax.random.normal(ks[1], (E, D), dtype=jnp.float32)).astype(bf)
        bias = jnp.zeros((E,), jnp.float32)
        W1 = (std * jax.random.normal(ks[2], (E, D, I), dtype=jnp.float32)).astype(bf)
        W3 = (std * jax.random.normal(ks[3], (E, D, I), dtype=jnp.float32)).astype(bf)
        W2 = (std * jax.random.normal(ks[4], (E, I, D), dtype=jnp.float32)).astype(bf)
        sw1 = (std * jax.random.normal(ks[5], (I, D), dtype=jnp.float32)).astype(bf)
        sw3 = (std * jax.random.normal(ks[6], (I, D), dtype=jnp.float32)).astype(bf)
        sw2 = (std * jax.random.normal(ks[7], (D, I), dtype=jnp.float32)).astype(bf)
        return {'x': x, 'gate_w': gate_w, 'bias': bias, 'W1': W1, 'W3': W3, 'W2': W2, 'sw1': sw1, 'sw3': sw3, 'sw2': sw2}
    _L0_ffn_all = _L0_ffn_setup()
    _L0_ffn_in = {k: v for k, v in _L0_ffn_all.items() if k in ('gate_w', 'bias', 'W1', 'W3', 'W2', 'sw1', 'sw3', 'sw2')}
    del _L0_ffn_all

    def _L1_xattn_setup():
        import jax, jax.numpy as jnp
        import numpy as np
        import math
        B, S, D, H = (4, 256, 128, 16)
        DV = D // H

        def _split_heads(x):
            b, s, _ = x.shape
            return x.reshape(b, s, H, DV).transpose(0, 2, 1, 3)
        key = jax.random.key(seed)
        ks = jax.random.split(key, 13)
        s = 1.0 / math.sqrt(D)
        inp = {'q': jax.random.normal(ks[0], (B, S, D), jnp.float32), 'k': jax.random.normal(ks[1], (B, S, D), jnp.float32), 'v': jax.random.normal(ks[2], (B, S, D), jnp.float32), 'mask': jax.random.bernoulli(ks[3], 0.1, (1, 1, S, S)), 'Wq': jax.random.normal(ks[4], (D, D), jnp.float32) * s, 'bq': jnp.zeros((D,), jnp.float32), 'Wk': jax.random.normal(ks[5], (D, D), jnp.float32) * s, 'bk': jnp.zeros((D,), jnp.float32), 'Wv': jax.random.normal(ks[6], (D, D), jnp.float32) * s, 'bv': jnp.zeros((D,), jnp.float32), 'Wo': jax.random.normal(ks[7], (D, D), jnp.float32) * s, 'bo': jnp.zeros((D,), jnp.float32)}
        return inp
    _L1_xattn_all = _L1_xattn_setup()
    _L1_xattn_in = {k: v for k, v in _L1_xattn_all.items() if k in ('Wq', 'bq', 'Wk', 'bk', 'Wv', 'bv', 'Wo', 'bo')}
    del _L1_xattn_all

    def _L1_ffn_setup():
        import jax, jax.numpy as jnp
        import numpy as np
        B, S, D, F, E = (4, 512, 128, 256, 8)
        key = jax.random.key(seed)
        ks = jax.random.split(key, 8)
        x = jax.random.normal(ks[0], (B, S, D), dtype=jnp.float32)
        Wr = jax.random.normal(ks[1], (D, E), dtype=jnp.float32) * 0.02
        br = jnp.zeros((E,), dtype=jnp.float32)
        W1 = jax.random.normal(ks[2], (E, D, F), dtype=jnp.float32) * (1.0 / np.sqrt(D))
        b1 = jnp.zeros((E, F), dtype=jnp.float32)
        W2 = jax.random.normal(ks[3], (E, F, D), dtype=jnp.float32) * (1.0 / np.sqrt(F))
        b2 = jnp.zeros((E, D), dtype=jnp.float32)
        return {'x': x, 'Wr': Wr, 'br': br, 'W1': W1, 'b1': b1, 'W2': W2, 'b2': b2}
    _L1_ffn_all = _L1_ffn_setup()
    _L1_ffn_in = {k: v for k, v in _L1_ffn_all.items() if k in ('Wr', 'br', 'W1', 'b1', 'W2', 'b2')}
    del _L1_ffn_all
    return {'x': x, 'ctx_1024': ctx_1024, 'mask_1x1xSxS2_ik0': mask_1x1xSxS2_ik0, 'mask_1x1xSxS2_bk0': mask_1x1xSxS2_bk0, 'L0_xattn_Wq': _L0_xattn_in['Wq'], 'L0_xattn_bq': _L0_xattn_in['bq'], 'L0_xattn_Wk': _L0_xattn_in['Wk'], 'L0_xattn_bk': _L0_xattn_in['bk'], 'L0_xattn_Wv': _L0_xattn_in['Wv'], 'L0_xattn_bv': _L0_xattn_in['bv'], 'L0_xattn_Wo': _L0_xattn_in['Wo'], 'L0_xattn_bo': _L0_xattn_in['bo'], 'L0_ffn_gate_w': _L0_ffn_in['gate_w'], 'L0_ffn_bias': _L0_ffn_in['bias'], 'L0_ffn_W1': _L0_ffn_in['W1'], 'L0_ffn_W3': _L0_ffn_in['W3'], 'L0_ffn_W2': _L0_ffn_in['W2'], 'L0_ffn_sw1': _L0_ffn_in['sw1'], 'L0_ffn_sw3': _L0_ffn_in['sw3'], 'L0_ffn_sw2': _L0_ffn_in['sw2'], 'L1_xattn_Wq': _L1_xattn_in['Wq'], 'L1_xattn_bq': _L1_xattn_in['bq'], 'L1_xattn_Wk': _L1_xattn_in['Wk'], 'L1_xattn_bk': _L1_xattn_in['bk'], 'L1_xattn_Wv': _L1_xattn_in['Wv'], 'L1_xattn_bv': _L1_xattn_in['bv'], 'L1_xattn_Wo': _L1_xattn_in['Wo'], 'L1_xattn_bo': _L1_xattn_in['bo'], 'L1_ffn_Wr': _L1_ffn_in['Wr'], 'L1_ffn_br': _L1_ffn_in['br'], 'L1_ffn_W1': _L1_ffn_in['W1'], 'L1_ffn_b1': _L1_ffn_in['b1'], 'L1_ffn_W2': _L1_ffn_in['W2'], 'L1_ffn_b2': _L1_ffn_in['b2']}

def reference(x, ctx_1024, mask_1x1xSxS2_ik0, mask_1x1xSxS2_bk0, L0_xattn_Wq, L0_xattn_bq, L0_xattn_Wk, L0_xattn_bk, L0_xattn_Wv, L0_xattn_bv, L0_xattn_Wo, L0_xattn_bo, L0_ffn_gate_w, L0_ffn_bias, L0_ffn_W1, L0_ffn_W3, L0_ffn_W2, L0_ffn_sw1, L0_ffn_sw3, L0_ffn_sw2, L1_xattn_Wq, L1_xattn_bq, L1_xattn_Wk, L1_xattn_bk, L1_xattn_Wv, L1_xattn_bv, L1_xattn_Wo, L1_xattn_bo, L1_ffn_Wr, L1_ffn_br, L1_ffn_W1, L1_ffn_b1, L1_ffn_W2, L1_ffn_b2):
    import jax
    import jax.numpy as jnp

    def _L0_xattn_ref(query, key, value, mask, Wq, bq, Wk, bk, Wv, bv, Wo, bo):
        import jax, jax.numpy as jnp
        import numpy as np
        D_MODEL = 128
        NUM_HEADS = 16
        HEAD_DIM = D_MODEL // NUM_HEADS
        B, S = (2, 256)
        b = query.shape[0]
        Q = query @ Wq + bq
        K = key @ Wk + bk
        V = value @ Wv + bv

        def split_heads(x):
            return x.reshape(b, -1, NUM_HEADS, HEAD_DIM).transpose(0, 2, 1, 3)
        Qh, Kh, Vh = (split_heads(Q), split_heads(K), split_heads(V))
        scores = jnp.einsum('bhqd,bhkd->bhqk', Qh, Kh) / jnp.sqrt(jnp.asarray(HEAD_DIM, jnp.float32))
        scores = jnp.where(mask == 0, jnp.asarray(-1e+20, scores.dtype), scores)
        weights = jax.nn.softmax(scores, axis=-1)
        attn = jnp.einsum('bhqk,bhkd->bhqd', weights, Vh)
        attn = attn.transpose(0, 2, 1, 3).reshape(b, -1, D_MODEL)
        return attn @ Wo + bo

    def _L0_ffn_ref(x, gate_w, bias, W1, W3, W2, sw1, sw3, sw2):
        import jax, jax.numpy as jnp
        import numpy as np
        D = 128
        I = 64
        E = 32
        K = 4
        T = 2 * 256
        C = 2 * T * K // E
        X = x.reshape(-1, D)
        logits = (X @ gate_w.T).astype(jnp.float32)
        scores = jax.nn.sigmoid(logits)
        _, idx = jax.lax.top_k(scores + bias[None, :], K)
        w = jnp.take_along_axis(scores, idx, axis=-1)
        w = w / jnp.clip(jnp.sum(w, axis=-1, keepdims=True), 1e-12, None)
        w = w.astype(x.dtype)
        eid = idx.reshape(-1)
        onehot = (eid[:, None] == jnp.arange(E)[None, :]).astype(jnp.int32)
        pos = jnp.take_along_axis(jnp.cumsum(onehot, axis=0) - 1, eid[:, None], axis=1)[:, 0]
        valid = pos < C
        posc = jnp.minimum(pos, C - 1)
        Xrep = jnp.repeat(X, K, axis=0)
        xe = jnp.zeros((E, C, D), x.dtype).at[eid, posc].add(jnp.where(valid[:, None], Xrep, jnp.zeros((), x.dtype)))
        h = jax.nn.silu(jnp.einsum('ecd,edi->eci', xe, W1)) * jnp.einsum('ecd,edi->eci', xe, W3)
        ye = jnp.einsum('eci,eid->ecd', h, W2)
        gflat = jnp.where(valid, w.reshape(-1), jnp.zeros((), x.dtype))
        yrows = ye[eid, posc] * gflat[:, None]
        out = yrows.reshape(-1, K, D).sum(axis=1)
        out = out + jax.nn.silu(X @ sw1.T) * (X @ sw3.T) @ sw2.T
        return out.reshape(x.shape)

    def _L1_xattn_ref(q, k, v, mask, Wq, bq, Wk, bk, Wv, bv, Wo, bo):
        import jax, jax.numpy as jnp
        import numpy as np
        import math
        B, S, D, H = (4, 256, 128, 16)
        DV = D // H

        def _split_heads(x):
            b, s, _ = x.shape
            return x.reshape(b, s, H, DV).transpose(0, 2, 1, 3)
        Q = _split_heads(q @ Wq.T + bq)
        K = _split_heads(k @ Wk.T + bk)
        V = _split_heads(v @ Wv.T + bv)
        scores = jnp.einsum('bhqd,bhkd->bhqk', Q, K) / math.sqrt(DV)
        scores = jnp.where(mask, jnp.asarray(1e-09, scores.dtype), scores)
        attn = jax.nn.softmax(scores, axis=-1)
        ctx = jnp.einsum('bhqk,bhkd->bhqd', attn, V)
        b = ctx.shape[0]
        ctx = ctx.transpose(0, 2, 1, 3).reshape(b, -1, H * DV)
        return ctx @ Wo.T + bo

    def _L1_ffn_ref(x, Wr, br, W1, b1, W2, b2):
        import jax, jax.numpy as jnp
        import numpy as np
        B, S, D, F, E = (4, 512, 128, 256, 8)
        logits = jnp.einsum('bsd,de->bse', x, Wr) + br
        probs = jax.nn.softmax(logits, axis=-1)
        expert_weights = jnp.max(probs, axis=-1)
        expert_indices = jnp.argmax(probs, axis=-1)
        num_experts = W1.shape[0]
        out = jnp.zeros_like(x)
        for e in range(num_experts):
            h = jax.nn.gelu(jnp.einsum('bsd,df->bsf', x, W1[e]) + b1[e], approximate=False)
            y = jnp.einsum('bsf,fd->bsd', h, W2[e]) + b2[e]
            out = jnp.where((expert_indices == e)[..., None], y, out)
        return out * expert_weights[..., None]
    x = x + _L0_xattn_ref(_layernorm(x, axis=-1), ctx_1024, ctx_1024, mask_1x1xSxS2_ik0, L0_xattn_Wq, L0_xattn_bq, L0_xattn_Wk, L0_xattn_bk, L0_xattn_Wv, L0_xattn_bv, L0_xattn_Wo, L0_xattn_bo)
    x = x + _L0_ffn_ref(_layernorm(x, axis=-1), L0_ffn_gate_w, L0_ffn_bias, L0_ffn_W1, L0_ffn_W3, L0_ffn_W2, L0_ffn_sw1, L0_ffn_sw3, L0_ffn_sw2)
    x = x + _L1_xattn_ref(_layernorm(x, axis=-1), ctx_1024, ctx_1024, mask_1x1xSxS2_bk0, L1_xattn_Wq, L1_xattn_bq, L1_xattn_Wk, L1_xattn_bk, L1_xattn_Wv, L1_xattn_bv, L1_xattn_Wo, L1_xattn_bo)
    x = x + _L1_ffn_ref(_layernorm(x, axis=-1), L1_ffn_Wr, L1_ffn_br, L1_ffn_W1, L1_ffn_b1, L1_ffn_W2, L1_ffn_b2)
    return x

_drawn_inputs = setup_inputs


def setup_inputs(seed=0):
    import zlib

    import numpy as np

    out = dict(_drawn_inputs(seed))
    spreads = {'L0_ffn_bias': (0.0, 0.8),
     'L1_xattn_bq': (0.0, 1.097),
     'L1_xattn_bk': (0.0, 2.0),
     'L1_xattn_bv': (0.0, 0.1),
     'L1_xattn_bo': (0.0, 0.1),
     'L1_ffn_br': (0.0, 0.1),
     'L1_ffn_b1': (0.0, 0.8),
     'L1_ffn_b2': (0.0, 0.57)}
    factors = {'L0_xattn_bq': 8.0,
     'L0_xattn_bk': 64.0,
     'L0_xattn_bo': 2.701,
     'L0_ffn_gate_w': 8.0,
     'L0_ffn_W1': 8.0,
     'L0_ffn_W3': 8.0,
     'L0_ffn_W2': 8.0,
     'L0_ffn_sw1': 8.0,
     'L0_ffn_sw3': 8.0,
     'L0_ffn_sw2': 8.0}
    for name, (base, spread) in spreads.items():
        noise = np.random.default_rng([zlib.crc32(name.encode()), seed]).standard_normal(out[name].shape)
        drawn = base * np.exp(spread * noise) if base else spread * noise
        out[name] = jnp.asarray(drawn.astype(out[name].dtype))
    for name, factor in factors.items():
        out[name] = (out[name] * factor).astype(out[name].dtype)
    return out
```

```python
from contextlib import ExitStack

import concourse.bass as bass
from concourse import mybir

ALU = mybir.AluOpType
ACT = mybir.ActivationFunctionType
AX = mybir.AxisListType
F32 = mybir.dt.float32
BF16 = mybir.dt.bfloat16
I32 = mybir.dt.int32
U32 = mybir.dt.uint32
U8 = mybir.dt.uint8

P = 128
NB = 32
S = 56
D = 128
H = 16
DH = D // H
SK = 1500
KT = 12
KP = SK // KT
HALF = 64
NS = NB // 2
HP = H // 2
HQ = HP * S
VW = DH + 1
VCOLS = 168
CHUNK = 4 * KP
SCALE = 1.0 / float(DH) ** 0.5
EPS = 1e-5
HIDE = -1e30
NONE = -3e38
E0, I0, TOPK, CAP = 32, 64, 4, 2 * 512 * 4 // 32
E1, F1 = 8, 256
TOKC = 4


class Tiles:
    pass


def above_zero(eng, sem, value):
    if isinstance(value, int) and value <= 0:
        return
    eng.wait_ge(sem, value)


def wait_apart(dve, T, sem, value):
    above_zero(dve, sem, value)
    dve.memset(T.carrier[:, :], 0.0)


def constants_and_loads(nc, ctx, A, T):
    sem = lambda n: ctx.enter_context(nc.semaphore(n))
    zeroed, loaded, made = sem("tiles_zeroed"), sem("inputs_loaded"), sem("constants_made")
    T.n_loads = 0
    with nc.Block() as block:

        @block.sync
        def _(sp):
            def load(dst, src):
                sp.dma_start(dst, src).then_inc(loaded, 16)
                T.n_loads += 1

            for j in range(2):
                load(T.w_in[:, j, 0], A[f"L{j}_xattn_Wq"])
                load(T.w_in[:, j, 1], A[f"L{j}_xattn_Wk"])
                load(T.w_in[:, j, 2], A[f"L{j}_xattn_Wv"])
                load(T.bq[:, j:j + 1], A[f"L{j}_xattn_bq"].rearrange("(n a) -> n a", a=1))
                load(T.bk[:, j:j + 1], A[f"L{j}_xattn_bk"].rearrange("(n a) -> n a", a=1))
                load(T.bv[:, j], A[f"L{j}_xattn_bv"].partition_broadcast(P))
                load(T.bo[:, j], A[f"L{j}_xattn_bo"].partition_broadcast(P))
            load(T.wo_in[:, :], A["L1_xattn_Wo"])
            load(T.gw_in[:, :], A["L0_ffn_gate_w"])
            load(T.sw1_in[:, :], A["L0_ffn_sw1"])
            load(T.sw3_in[:, :], A["L0_ffn_sw3"])
            load(T.sw2_in[:, :], A["L0_ffn_sw2"])
            load(T.ebias[:, :], A["L0_ffn_bias"].partition_broadcast(P))
            load(T.wr[:, :], A["L1_ffn_Wr"])
            load(T.br[:, :], A["L1_ffn_br"].partition_broadcast(P))
            load(T.b2[:, :], A["L1_ffn_b2"])
            sp.wait_ge(zeroed, 8)
            for par in range(2):
                rows = slice(HALF * par, HALF * par + S)
                load(T.x[rows, :, :], A["x"].rearrange("(i two) q d -> two q i d", two=2)[par])
                load(T.mask0[rows, :], A["mask_1x1xSxS2_ik0"][0, 0])
                load(T.mask1[rows, :], A["mask_1x1xSxS2_bk0"][0, 0])
            wo = A["L0_xattn_Wo"]
            for g in range(4):
                for j in range(4):
                    h = 3 * g + j if j < 3 else 12 + g
                    r = 32 * g + (VW * j if j < 3 else 0)
                    load(T.wo[r:r + DH, 0, j, :], wo[DH * h:DH * h + DH, :])
            with nc.allow_non_contiguous_dma(reason="expert weights, once"):
                load(T.w1[0][:, 0:16, :].rearrange("p u (j i) -> p (u j) i", j=2),
                     A["L0_ffn_W1"].rearrange("e d i -> d e i"))
                load(T.w3[:, 0:16, :].rearrange("p u (j i) -> p (u j) i", j=2),
                     A["L0_ffn_W3"].rearrange("e d i -> d e i"))
                load(T.w2[0][:, 0:16, :], A["L0_ffn_W2"].rearrange("(u j) i d -> (j i) u d", j=2))
                load(T.w1[1][:, :, :].rearrange("p (e a) f -> p e (a f)", a=2),
                     A["L1_ffn_W1"].rearrange("e d f -> d e f"))
                load(T.w2[1][:, :, :].rearrange("p (e a) d -> p e a d", a=2),
                     A["L1_ffn_W2"].rearrange("e (a f) d -> f e a d", a=2))
                load(T.b1[:, :, 0], A["L1_ffn_b1"].rearrange("e (a f) -> f (e a)", a=2))
            sp.wait_ge(loaded, 16 * T.n_loads)

        @block.vector
        def _(dve):
            for tile, value in ((T.x, 0.0), (T.mask0, 1), (T.mask1, 0), (T.wo, 0.0), (T.w1[0], 0.0),
                                (T.w3, 0.0), (T.w2[0], 0.0), (T.gateT, 0.0)):
                dve.memset(tile[:], value).then_inc(zeroed, 1)
            for tile in (T.v[0], T.v[1], T.mv9[0], T.mv9[1], T.gt, T.mvr[0], T.mvr[1],
                         T.de[0], T.de[1], T.qbf, T.woa):
                dve.memset(tile[:], 0.0).then_inc(zeroed, 1)
            dve.memset(T.ones_b[:], 1.0)
            dve.wait_ge(zeroed, 19)
            dve.memset(T.gateT[32:64, :], 1.0)
            for v in T.v:
                dve.memset(v[:, :, 0:H * VW].rearrange("p t (h d) -> p t h d", d=VW)[:, :, :, DH:VW], 1.0)

        @block.gpsimd
        def _(pool):
            n = [0]

            def made_by(ins):
                ins.then_inc(made, 1)
                n[0] += 1
                pool.wait_ge(made, n[0])

            def one_where_zero(tile, base, pattern, mult=1):
                made_by(pool.memset(tile, 0.0))
                made_by(pool.affine_select(out=tile, in_=tile, compare_op=ALU.not_equal, fill=1.0,
                                           base=base, pattern=pattern, channel_multiplier=mult))

            one_where_zero(T.ident[:, :], 0, [[-1, P]])
            one_where_zero(T.ident_b[:, :], 0, [[-1, P]])
            made_by(pool.memset(T.headmask[:, :], 1.0))
            made_by(pool.affine_select(out=T.headmask[:, :], in_=T.headmask[:, :], compare_op=ALU.is_ge,
                                       fill=0.0, base=0, pattern=[[-DH, H]], channel_multiplier=1))
            made_by(pool.affine_select(out=T.headmask[:, :], in_=T.headmask[:, :], compare_op=ALU.is_ge,
                                       fill=0.0, base=DH - 1, pattern=[[DH, H]], channel_multiplier=-1))
            for j in range(4):
                first = VW * j + DH if j < 3 else DH
                one_where_zero(T.densel[:, j, :], -first, [[-32, 4], [0, 32]])
            one_where_zero(T.pick[0][:, :, :], 0, [[-2, 17], [-1, 2], [0, 64]])
            one_where_zero(T.pick[1][:, :, :], 0, [[-1, 8], [0, 2], [0, P]])
            made_by(pool.memset(T.earlier[:, :], 1.0))
            made_by(pool.affine_select(out=T.earlier[:, :], in_=T.earlier[:, :], compare_op=ALU.is_gt,
                                       fill=0.0, base=0, pattern=[[1, P]], channel_multiplier=-1))
            made_by(pool.iota(T.iota_i[:, :], pattern=[[1, E0]], base=0, channel_multiplier=0))
            made_by(pool.tensor_copy(T.iota_f[:, :], T.iota_i[:, :]))
            made_by(pool.memset(T.turn[:, :], 0.0))
            made_by(pool.memset(T.rowvalid[:, :], 0.0))
            for par in range(2):
                pool.memset(T.idq[:, :], 0.0) if par == 0 else None
                made_by(pool.memset(T.rowvalid[HALF * par:HALF * par + S, :], 1.0))
            made_by(pool.tensor_tensor(T.idq[:, :], T.ident[:, 0:S], T.ident[:, HALF:HALF + S], ALU.add))


def prepare(nc, ctx, A, T):
    sem = lambda n: ctx.enter_context(nc.semaphore(n))
    turned, masks_made, step = sem("weights_turned"), sem("masks_made"), sem("prepare_step")
    big = [T.psum[:, b, :] for b in range(8)]
    with nc.Block() as block:

        @block.tensor
        def _(pe):
            for k in range(3):
                pe.transpose(big[0][:, P * k:P * k + P], T.w_in[:, 1, k], T.ident[:, :])
            pe.matmul(big[2][:, 0:E0], T.gw_in[:, :], T.ident_b[0:E0, 0:E0], start=True, stop=True)
            pe.matmul(big[2][:, 64:64 + I0], T.sw1_in[:, :], T.ident_b[0:I0, 0:I0], start=True, stop=True)
            pe.matmul(big[2][:, 128:128 + I0], T.sw3_in[:, :], T.ident_b[0:I0, 0:I0], start=True, stop=True)
            pe.matmul(big[3][0:I0, 0:D], T.sw2_in[:, :], T.ident_b[:, :], start=True, stop=True)
            pe.wait_ge(masks_made, 1)
            for j in range(4):
                pe.transpose(big[1][:, P * j:P * j + P], T.woa[:, j, :], T.ident[:, :])
            pe.wait_ge(masks_made, 3)
            for layer in range(2):
                for t in range(KT):
                    ins = pe.matmul(big[4 + 2 * layer + t // 6][0:KP, S * (t % 6):S * (t % 6) + S],
                                    T.mk[0:S, layer, KP * t:KP * t + KP], T.ident_b[0:S, 0:S],
                                    start=True, stop=True)
            ins.then_inc(turned, 1)

        @block.vector
        def _(dve):
            n = [0]

            def after(ins):
                ins.then_inc(step, 1)
                n[0] += 1
                dve.wait_ge(step, n[0])

            for j in range(4):
                src = T.wo_in[:, 0:96] if j < 3 else T.wo_in[:, 96:128]
                if j < 3:
                    src = src.rearrange("p (g k d) -> p g k d", g=4, k=3)[:, :, j, :]
                else:
                    src = src.rearrange("p (g d) -> p g d", g=4)
                off = VW * j if j < 3 else 0
                dst = T.woa[:, j, :].rearrange("p (g r) -> p g r", g=4)[:, :, off:off + DH]
                ins = dve.tensor_copy(dst, src)
            ins.then_inc(masks_made, 1)
            for layer in range(2):
                src = (T.mask0 if layer == 0 else T.mask1.bitcast(U8))[:, :].rearrange("q (p t) -> q t p", t=KT)
                dst = T.mk[:, layer, :].rearrange("q (t p) -> q t p", t=KT)
                dve.tensor_scalar(dst, src, 0.0, None, ALU.is_equal if layer == 0 else ALU.not_equal)\
                   .then_inc(masks_made, 1)
            dve.wait_ge(masks_made, 3)
            for layer in range(2):
                masked = T.mk[:, layer, :]
                after(dve.tensor_scalar(T.hide[:, layer, :], masked, HIDE, None, ALU.mult))
                after(dve.tensor_reduce(T.count[:, layer:layer + 1], masked, AX.X, ALU.add))
                after(dve.tensor_reduce(T.floor[:, layer:layer + 1], masked, AX.X, ALU.max))
                after(dve.tensor_scalar(T.tmp1[:, :], T.floor[:, layer:layer + 1], -1.0, -NONE,
                                        ALU.add, ALU.mult))
                after(dve.scalar_tensor_tensor(out=T.floor[:, layer:layer + 1],
                                               in0=T.floor[:, layer:layer + 1], scalar=T.masked[layer],
                                               in1=T.tmp1[:, :], op0=ALU.mult, op1=ALU.add))
                after(dve.tensor_scalar(T.countbv[:, layer, :], T.bv[:, layer, :],
                                        T.count[:, layer:layer + 1], None, ALU.mult))
                after(dve.tensor_scalar(T.bq[:, layer:layer + 1], T.bq[:, layer:layer + 1], SCALE, None, ALU.mult))
                after(dve.memset(T.shiftw[:, layer, :, :], 1.0))
                dve.tensor_copy(T.shiftw[HALF:P, layer, 0, :], T.hide[HALF:P, layer, :])
                after(dve.tensor_copy(T.shiftw[0:HALF, layer, 1, :], T.hide[0:HALF, layer, :]))
            for par in range(2):
                for p in range(HP):
                    dve.tensor_copy(T.mvr[par][HALF:HALF + S, 0, p, :], T.idq[HALF:HALF + S, :])
                    after(dve.tensor_copy(T.mvr[par][0:S, 1, p, :], T.idq[0:S, :]))
            dve.wait_ge(turned, 1)
            after(dve.tensor_copy(T.w_t[:, 1].rearrange("p k n -> p (k n)"), big[0][:, 0:3 * P]))
            after(dve.tensor_copy(T.w_t[:, 0], T.w_in[:, 0]))
            after(dve.tensor_copy(T.wo[:, 1].rearrange("p j n -> p (j n)"), big[1][:, :]))
            after(dve.tensor_copy(T.gw[:, :], big[2][:, 0:E0]))
            after(dve.tensor_copy(T.w1[0][:, 16, 0:I0], big[2][:, 64:64 + I0]))
            after(dve.tensor_copy(T.w3[:, 16, 0:I0], big[2][:, 128:128 + I0]))
            after(dve.tensor_copy(T.w2[0][0:I0, 16, :], big[3][0:I0, 0:D]))
            for layer in range(2):
                for half in range(2):
                    after(dve.tensor_copy(
                        T.mkT[0:KP, layer, 6 * half:6 * half + 6, :],
                        big[4 + 2 * layer + half][0:KP, 0:6 * S].rearrange("p (t q) -> p t q", t=6)))


def normalise(nc, ctx, T, name):
    sem = lambda n: ctx.enter_context(nc.semaphore(f"{name}_{n}"))
    stats_done, moments_done, std_done, xn_done = sem("stats"), sem("moments"), sem("std"), sem("xn")
    step, turned, copied = sem("step"), sem("turned"), sem("copied")
    with nc.Block() as block:

        @block.vector
        def _(dve):
            for i in range(NS):
                dve.bn_stats(T.stats[:, i, :], T.x[:, i, :]).then_inc(stats_done, 1)
                dve.wait_ge(stats_done, i + 1)
                dve.bn_aggr(T.moments[:, i, :], T.stats[:, i, :]).then_inc(moments_done, 1)
            dve.wait_ge(moments_done, NS)
            dve.tensor_scalar(T.var[:, :], T.moments[:, :, 1], EPS, None, ALU.add).then_inc(step, 1)
            dve.wait_ge(std_done, 1)
            dve.reciprocal(T.rstd[:, :, 0], T.std[:, :]).then_inc(step, 1)
            dve.wait_ge(step, 2)
            with dve.Fori(0, NS) as i:
                dve.tensor_scalar(T.xn[:, i, :], T.x[:, i, :], T.moments[:, i, 0:1], T.rstd[:, i, :],
                                  ALU.subtract, ALU.mult).then_inc(xn_done, 1)

        @block.scalar
        def _(act):
            act.wait_ge(step, 1)
            act.activation(T.std[:, :], T.var[:, :], ACT.Sqrt).then_inc(std_done, 1)
            for b in range(4):
                act.wait_ge(turned, b + 1)
                act.activation(T.xT[:, 4 * b:4 * b + 4, :].rearrange("p i t -> p (i t)"),
                               T.psum[:, b, :], ACT.Copy).then_inc(copied, 1)

        @block.tensor
        def _(pe):
            for i in range(NS):
                pe.wait_ge(xn_done, i + 1)
                ins = pe.transpose(T.psum[:, i // 4, P * (i % 4):P * (i % 4) + P], T.xn[:, i, :], T.ident[:, :])
                if i % 4 == 3:
                    ins.then_inc(turned, 1)


def queries(nc, ctx, T, layer):
    sem = lambda n: ctx.enter_context(nc.semaphore(f"q{layer}_{n}"))
    projected, done = sem("projected"), sem("done")
    with nc.Block() as block:

        @block.tensor
        def _(pe):
            for b in range(4):
                pe.matmul(T.psum[:, b, :], T.w_t[:, layer, 0], T.xT[:, 4 * b:4 * b + 4, :].rearrange("p i t -> p (i t)"),
                          start=True, stop=True).then_inc(projected, 1)

        @block.scalar
        def _(act):
            for b in range(4):
                act.wait_ge(projected, b + 1)
                act.activation(T.qT[:, 4 * b:4 * b + 4, :].rearrange("p i t -> p (i t)"), T.psum[:, b, :],
                               ACT.Identity, bias=T.bq[:, layer:layer + 1], scale=SCALE).then_inc(done, 1)

        @block.vector
        def _(dve):
            dve.tensor_tensor(T.x[:, :, :], T.x[:, :, :],
                              T.bo[:, layer, :].unsqueeze(1).to_broadcast([P, NS, D]), ALU.add).then_inc(done, 1)


def attention(nc, ctx, A, T, layer):
    sem = lambda n: ctx.enter_context(nc.semaphore(f"a{layer}_{n}"))
    ctx_landed = [sem("ctx_landed0"), sem("ctx_landed1")]
    ctxT_ready, ctxT_copied = sem("ctxT_ready"), sem("ctxT_copied")
    k_ready, k_copied = sem("k_ready"), sem("k_copied")
    v_ready, v_copied = sem("v_ready"), sem("v_copied")
    g_ready, g_copied, mv_ready, mv_copied = sem("g_ready"), sem("g_copied"), sem("mv_ready"), sem("mv_copied")
    q_ready = sem("q_ready")
    first_ready, max_taken, floor_taken = sem("first_ready"), sem("max_taken"), sem("floor_taken")
    negm_ready, earg_ready, shift_ready, emask_ready, de_ready = sem("negm_ready"), sem("earg_ready"), sem("shift_ready"), sem("emask_ready"), sem("de_ready")
    scores_ready, probs_ready, probs_used = sem("scores_ready"), sem("probs_ready"), sem("probs_used")
    sums_ready, sums_copied, den_ready, recip_ready = sem("sums_ready"), sem("sums_copied"), sem("den_ready"), sem("recip_ready")
    attn_ready, out_ready, x_added = sem("attn_ready"), sem("out_ready"), sem("x_added")
    ctx_dram = A["ctx_1024"].rearrange("b (p t) d -> b p t d", t=KT)
    bank = [T.psum[:, j, :] for j in range(3)]
    three = T.psum[:, 0:3, 0:CHUNK]
    scores_ps = [T.psum[:, 3:5, 0:HQ], T.psum[:, 5:7, 0:HQ]]
    sums_ps = T.psum[:, 7, 0:4 * S]
    wk, wv = T.w_t[:, layer, 1], T.w_t[:, layer, 2]

    def steps(eng, step):
        step(0, 0, True, False)
        step(0, 1, False, False)
        with eng.Fori(1, NS - 1) as i:
            step(i, 0, False, False)
            step(i, 1, False, False)
        step(NS - 1, 0, False, False)
        step(NS - 1, 1, False, True)

    def after(i, par):
        return (i, 1) if par == 0 else (i + 1, 0)

    with nc.Block() as block:

        @block.sync
        def _(sp):
            for b in range(2):
                sp.dma_start(T.ctx[b][0:KP], ctx_dram[b]).then_inc(ctx_landed[b], 16)
            with sp.Fori(1, NS) as i:
                for par in range(2):
                    sp.wait_ge(g_ready, 2 * i + par - 1)
                    sp.dma_start(T.ctx[par][0:KP], ctx_dram[2 * i + par]).then_inc(ctx_landed[par], 16)

        @block.tensor
        def _(pe):
            def turn(i, par, j, to):
                if j == 0:
                    pe.wait_ge(ctx_landed[par], 16 * i + 16)
                for u in range(4):
                    ins = pe.transpose(bank[to][:, KP * u:KP * u + KP], T.ctx[par][0:KP, 4 * j + u, :],
                                       T.ident[0:KP, 0:KP])
                ins.then_inc(ctxT_ready, 1)

            def keys(n, j, to):
                pe.wait_ge(ctxT_copied, 3 * n + j + 1)
                pe.matmul(bank[to][:, 0:CHUNK], wk, T.ctxT[:, CHUNK * j:CHUNK * j + CHUNK],
                          start=True, stop=True).then_inc(k_ready, 1)

            def values(j, to):
                for u in range(4):
                    t = 4 * j + u
                    ins = pe.matmul(bank[to][0:KP, P * u:P * u + P], T.ctxT[:, KP * t:KP * t + KP], wv,
                                    start=True, stop=True)
                ins.then_inc(v_ready, 1)

            def masked_context(par, to):
                for t in range(KT):
                    ins = pe.matmul(bank[to][:, 0:S], T.ctx[par][0:KP, t, :], T.mkT[0:KP, layer, t, :],
                                    start=(t == 0), stop=(t == KT - 1))
                ins.then_inc(g_ready, 1)

            def masked_values(n, to):
                pe.wait_ge(g_copied, n + 1)
                pe.matmul(bank[to][:, 0:D], T.gt[:, :], wv, start=True, stop=True).then_inc(mv_ready, 1)

            def first_pass(n, p):
                if p == 0:
                    pe.wait_ge(k_copied, 3 * n + 3)
                    pe.wait_ge(q_ready, n + 1)
                else:
                    pe.wait_ge(max_taken, 8 * n + p)
                for j in range(3):
                    ins = pe.matmul(T.psum[:, j, 0:CHUNK], T.qbf[:, p].rearrange("k a q -> k (a q)"),
                                    T.kbf[:, CHUNK * j:CHUNK * j + CHUNK], start=True, stop=True)
                ins.then_inc(first_ready, 1)

            def prepare_next(n, i, par, t, late):
                if t == 0 and not late:
                    turn(i, par, 0, 1)
                    turn(i, par, 1, 2)
                if t == 1 and not late:
                    above_zero(pe, recip_ready, n - 1)
                    turn(i, par, 2, 0)
                    keys(n, 0, 1)
                    keys(n, 1, 2)
                if t == 2 and late:
                    pe.wait_ge(ctxT_copied, 3 * n + 3)
                    pe.wait_ge(k_copied, 3 * n + 1)
                    keys(n, 2, 1)
                    pe.wait_ge(k_copied, 3 * n + 2)
                    values(0, 2)
                if t == 3 and not late:
                    above_zero(pe, x_added, n - 1)
                    values(1, 0)
                    pe.wait_ge(k_copied, 3 * n + 3)
                    values(2, 1)
                if t == 3 and late:
                    pe.wait_ge(v_copied, 3 * n + 1)
                    masked_context(par, 2)
                if t == 4 and late:
                    pe.wait_ge(v_copied, 3 * n + 2)
                    masked_values(n, 0)
                if 5 <= t < 9:
                    if t == 5 and not late:
                        pe.wait_ge(v_copied, 3 * n + 3)
                        pe.wait_ge(mv_copied, n + 1)
                    first_pass(n, 2 * (t - 5) + late)

            def scores(b, i, par, t):
                if t == 0:
                    pe.wait_ge(shift_ready, 2 * (b + 1))
                m = KT * b + t
                above_zero(pe, probs_ready, m - 1)
                for a in range(2):
                    pe.matmul(scores_ps[t % 2][0:KP, a, :], T.k[par][:, KP * t:KP * t + KP],
                              T.qblk[par][:, HP * a:HP * a + HP, :].rearrange("k h q -> k (h q)"),
                              start=True, stop=False)
                    ins = pe.matmul(scores_ps[t % 2][0:KP, a, :], T.shiftw[:, layer, a, KP * t:KP * t + KP],
                                    T.mvr[par][:, a].rearrange("r p q -> r (p q)"), start=False, stop=True)
                ins.then_inc(scores_ready, 1)

            def weigh(values_of, weights, start, stop):
                for g in range(4):
                    pe.matmul(sums_ps[32 * g:32 * g + 32, 0:3 * S], values_of(3 * VW * g),
                              weights[:, 3 * S * g:3 * S * g + 3 * S], start=start, stop=stop,
                              skip_group_check=True)
                for g in range(4):
                    ins = pe.matmul(sums_ps[32 * g:32 * g + 32, 3 * S:4 * S], values_of(12 * VW + VW * g),
                                    weights[:, S * (12 + g):S * (12 + g) + S], start=False, stop=stop,
                                    skip_group_check=True)
                return ins

            def weigh_tile(b, par, t):
                pe.wait_ge(probs_ready, KT * b + t + 1)
                if t == 0:
                    above_zero(pe, sums_copied, b)
                weigh(lambda c: T.v[par][0:KP, t, c:c + 32], T.probs[t % 3][0:KP, :], t == 0, False)\
                    .then_inc(probs_used, 1)

            def weigh_masked(b, par):
                pe.wait_ge(de_ready, 2 * (b + 1))
                weigh(lambda c: T.mv9[par][:, c:c + 32], T.de[par][:, :, :].rearrange("r h q -> r (h q)"),
                      False, True).then_inc(sums_ready, 1)

            def denominators(b):
                pe.wait_ge(sums_copied, b + 1)
                pe.wait_ge(max_taken, 8 * (b + 2)) if b_not_last[0] else None
                for j in range(4):
                    ins = pe.matmul(bank[0][:, S * j:S * j + S], T.densel[:, j, :], T.sums[:, S * j:S * j + S],
                                    start=True, stop=True)
                ins.then_inc(den_ready, 1)

            def project(b, i, par):
                pe.wait_ge(attn_ready, b + 1)
                rows = slice(HALF * par, HALF * par + S)
                for j in range(4):
                    ins = pe.matmul(bank[0][rows, 0:D], T.attn[:, S * j:S * j + S], T.wo[:, layer, j, :],
                                    start=(j == 0), stop=(j == 3))
                ins.then_inc(out_ready, 1)

            b_not_last = [True]
            for t in range(KT):
                for late in (False, True):
                    prepare_next(0, 0, 0, t, late)

            def step(i, par, first, last):
                b = 2 * i + par
                ni, npar = after(i, par)
                for t in range(KT):
                    scores(b, i, par, t)
                    if t == 0:
                        pe.wait_ge(max_taken, 8 * (b + 1))
                    if t > 0:
                        if not last:
                            prepare_next(b + 1, ni, npar, t, False)
                        weigh_tile(b, par, t - 1)
                    elif not first:
                        weigh_tile(b - 1, 1 - par, KT - 1)
                        weigh_masked(b - 1, 1 - par)
                        if not last:
                            prepare_next(b + 1, ni, npar, t, False)
                        denominators(b - 1)
                    elif not last:
                        prepare_next(b + 1, ni, npar, t, False)
                    if t == 2 and not first:
                        if not last:
                            pe.wait_ge(ctxT_copied, 3 * (b + 1) + 3)
                        else:
                            pe.wait_ge(recip_ready, b)
                        project(b - 1, *((i, 0) if par else (i - 1, 1)))
                    if not last:
                        prepare_next(b + 1, ni, npar, t, True)
                if last:
                    weigh_tile(b, par, KT - 1)
                    weigh_masked(b, par)
                    b_not_last[0] = False
                    pe.wait_ge(x_added, b)
                    denominators(b)
                    pe.wait_ge(recip_ready, b + 1)
                    project(b, i, par)

            steps(pe, step)

        @block.scalar
        def _(act):
            def copy_turned(n, j, src):
                if j == 0:
                    above_zero(act, v_ready, 3 * n)
                act.wait_ge(ctxT_ready, 3 * n + j + 1)
                act.activation(T.ctxT[:, CHUNK * j:CHUNK * j + CHUNK], bank[src][:, 0:CHUNK], ACT.Copy)\
                   .then_inc(ctxT_copied, 1)

            def copy_keys(n, par, j, src):
                act.wait_ge(k_ready, 3 * n + j + 1)
                act.activation(T.k[par][:, CHUNK * j:CHUNK * j + CHUNK], bank[src][:, 0:CHUNK], ACT.Identity,
                               bias=T.bk[:, layer:layer + 1])
                above_zero(act, first_ready, 8 * n)
                act.activation(T.kbf[:, CHUNK * j:CHUNK * j + CHUNK], bank[src][:, 0:CHUNK], ACT.Identity,
                               bias=T.bk[:, layer:layer + 1]).then_inc(k_copied, 1)

            def prepare_next(n, par, t):
                if t == 0:
                    copy_turned(n, 0, 1)
                    copy_turned(n, 1, 2)
                if t == 1:
                    copy_turned(n, 2, 0)
                    copy_keys(n, par, 0, 1)
                    copy_keys(n, par, 1, 2)
                if t == 2:
                    copy_keys(n, par, 2, 1)
                if t == 9:
                    act.wait_ge(earg_ready, n + 1)
                    above_zero(act, de_ready, 2 * n)
                    act.activation(T.emask[:, :], T.earg[:, :], ACT.Exp).then_inc(emask_ready, 1)

            for t in range(KT):
                prepare_next(0, 0, t)

            def copy_sums(b):
                act.wait_ge(sums_ready, b + 1)
                above_zero(act, attn_ready, b)
                act.activation(T.sums[:, :], sums_ps, ACT.Copy).then_inc(sums_copied, 1)

            def step(i, par, first, last):
                b = 2 * i + par
                for t in range(KT):
                    m = KT * b + t
                    act.wait_ge(scores_ready, m + 1)
                    above_zero(act, probs_used, m - 2)
                    act.activation(T.probs[t % 3][0:KP, :].rearrange("k (a c) -> k a c", a=2),
                                   scores_ps[t % 2][0:KP], ACT.Exp).then_inc(probs_ready, 1)
                    if t == 0 and not first:
                        copy_sums(b - 1)
                    if not last:
                        prepare_next(b + 1, 1 - par, t)
                if last:
                    copy_sums(b)

            steps(act, step)

        @block.vector
        def _(dve):
            def prepare_next(n, par):
                v4 = T.v[par][:, :, 0:H * VW].rearrange("k t (h d) -> k t h d", d=VW)
                for j, src in ((0, 2), (1, 0), (2, 1)):
                    dve.wait_ge(v_ready, 3 * n + j + 1)
                    dve.tensor_tensor(v4[0:KP, 4 * j:4 * j + 4, :, 0:DH],
                                      bank[src][0:KP, :].rearrange("k (t h d) -> k t h d", t=4, h=H),
                                      T.bv[0:KP, layer, :].rearrange("k (h d) -> k h d", d=DH).unsqueeze(1)
                                      .to_broadcast([KP, 4, H, DH]), ALU.add).then_inc(v_copied, 1)
                dve.wait_ge(g_ready, n + 1)
                dve.tensor_copy(T.gt[:, 0:S], bank[2][:, 0:S])
                dve.tensor_copy(T.gt[:, HALF:HALF + S], bank[2][:, 0:S]).then_inc(g_copied, 1)
                dve.wait_ge(mv_ready, n + 1)
                dve.tensor_tensor(T.mv9[par][:, 0:H * VW].rearrange("q (h d) -> q h d", d=VW)[:, :, 0:DH],
                                  bank[0][:, 0:D].rearrange("q (h d) -> q h d", d=DH),
                                  T.countbv[:, layer, :].rearrange("q (h d) -> q h d", d=DH), ALU.add)\
                   .then_inc(mv_copied, 1)
                for p in range(HP):
                    wait_apart(dve, T, first_ready, 8 * n + p + 1)
                    dve.tensor_tensor_reduce(out=T.junk[:, :].rearrange("q (j k) -> q j k", j=3), in0=three,
                                             in1=T.hide[:, layer, :].rearrange("q (j k) -> q j k", j=3),
                                             scale=1.0, scalar=NONE, op0=ALU.add, op1=ALU.max,
                                             accum_out=T.rowmax[:, p:p + 1]).then_inc(max_taken, 1)
                dve.wait_ge(max_taken, 8 * n + 8)
                above_zero(dve, de_ready, 2 * n)
                dve.tensor_scalar(T.negm[:, :], T.rowmax[:, :], T.floor[:, layer:layer + 1], -1.0,
                                  ALU.max, ALU.mult).then_inc(negm_ready, 1)
                dve.wait_ge(negm_ready, n + 1)
                dve.tensor_scalar(T.earg[:, :], T.negm[:, :], T.masked[layer], 0.0, ALU.add, ALU.min)\
                   .then_inc(earg_ready, 1)
                for a in range(2):
                    rows = slice(HALF * a, HALF * a + S)
                    dve.tensor_tensor(T.mvr[par][rows, a, :, :],
                                       T.idq[rows, :].unsqueeze(1).to_broadcast([S, HP, S]),
                                       T.negm[rows, :].unsqueeze(2).to_broadcast([S, HP, S]), ALU.mult)\
                        .then_inc(shift_ready, 1)
                above_zero(dve, sums_ready, n - 1)
                dve.wait_ge(emask_ready, n + 1)
                for a in range(2):
                    rows = slice(HALF * a, HALF * a + S)
                    dve.tensor_tensor(T.de[par][rows, HP * a:HP * a + HP, :],
                                       T.idq[rows, :].unsqueeze(1).to_broadcast([S, HP, S]),
                                       T.emask[rows, :].unsqueeze(2).to_broadcast([S, HP, S]), ALU.mult)\
                        .then_inc(de_ready, 1)

            def divide(b):
                dve.wait_ge(den_ready, b + 1)
                dve.reciprocal(T.recip[:, :], bank[0][:, 0:4 * S]).then_inc(recip_ready, 1)
                dve.wait_ge(recip_ready, b + 1)
                dve.tensor_tensor(T.attn[:, :], T.sums[:, :], T.recip[:, :], ALU.mult).then_inc(attn_ready, 1)

            def add_to_x(b, i, par):
                rows = slice(HALF * par, HALF * par + S)
                dve.wait_ge(out_ready, b + 1)
                dve.tensor_tensor(T.x[rows, i, :], T.x[rows, i, :], bank[0][rows, 0:D], ALU.add)\
                   .then_inc(x_added, 1)

            for par in range(2):
                dve.tensor_copy(T.mv9[par][:, 0:H * VW].rearrange("q (h d) -> q h d", d=VW)[:, :, DH:VW],
                                T.count[:, layer:layer + 1].unsqueeze(1).to_broadcast([P, H, 1]))
            prepare_next(0, 0)

            def step(i, par, first, last):
                b = 2 * i + par
                if not first:
                    divide(b - 1)
                    add_to_x(b - 1, *((i, 0) if par else (i - 1, 1)))
                if not last:
                    prepare_next(b + 1, 1 - par)
                else:
                    divide(b)
                    add_to_x(b, i, par)

            steps(dve, step)

        @block.gpsimd
        def _(pool):
            def prepare_next(n, i, par):
                above_zero(pool, scores_ready, KT * (n - 1))
                above_zero(pool, first_ready, 8 * n)
                pool.tensor_tensor(T.turn[:, :], T.turn[:, :], T.turn[:, :], ALU.mult)
                q = T.qT[:, i, HALF * par:HALF * par + S]
                pool.tensor_tensor(T.qblk[par][:, :, :], q.unsqueeze(1).to_broadcast([P, H, S]),
                                   T.headmask[:, :].unsqueeze(2).to_broadcast([P, H, S]), ALU.mult)
                for a in range(2):
                    ins = pool.tensor_tensor(T.qbf[:, :, a, 0:S], q.unsqueeze(1).to_broadcast([P, HP, S]),
                                             T.headmask[:, HP * a:HP * a + HP].unsqueeze(2).to_broadcast([P, HP, S]),
                                             ALU.mult)
                ins.then_inc(q_ready, 1)

            prepare_next(0, 0, 0)

            def step(i, par, first, last):
                if not last:
                    prepare_next(2 * i + par + 1, *after(i, par))

            steps(pool, step)


def gates0(nc, ctx, T):
    sem = lambda n: ctx.enter_context(nc.semaphore(f"g0_{n}"))
    logits, scored, step, chosen, counted, gated, turned = (
        sem("logits"), sem("scored"), sem("step"), sem("chosen"), sem("counted"), sem("gated"), sem("turned"))
    top_done, idx_done = sem("top"), sem("idx")
    flat = lambda t: t.rearrange("p i e -> p (i e)")
    with nc.Block() as block:

        @block.tensor
        def _(pe):
            for i in range(NS):
                ins = pe.matmul(T.psum[:, 0, E0 * i:E0 * i + E0], T.xT[:, i, :], T.gw[:, :], start=True, stop=True)
            ins.then_inc(logits, 1)
            pe.wait_ge(chosen, 1)
            pe.matmul(T.psum[:, 1, :], T.earlier[:, :], flat(T.sel_b[:, :, :]), start=True, stop=True)
            pe.matmul(T.psum[:, 2, :], T.ones_b[:, :], flat(T.sel_b[:, :, :]), start=True, stop=True)\
              .then_inc(counted, 1)
            pe.wait_ge(gated, 1)
            for i in range(NS):
                ins = pe.transpose(T.psum[0:E0, 4 + i // 4, P * (i % 4):P * (i % 4) + P], T.gate[:, i, :],
                                   T.ident[:, :])
            ins.then_inc(turned, 1)

        @block.scalar
        def _(act):
            act.wait_ge(logits, 1)
            act.activation(flat(T.score[:, :, :]), T.psum[:, 0, :], ACT.Sigmoid).then_inc(scored, 1)
            act.wait_ge(turned, 1)
            for b in range(4):
                act.activation(T.gateT[0:E0, P * 4 * b:P * 4 * b + 4 * P], T.psum[0:E0, 4 + b, :], ACT.Copy)

        @block.vector
        def _(dve):
            n = [0]

            def after(ins):
                ins.then_inc(step, 1)
                n[0] += 1
                dve.wait_ge(step, n[0])

            dve.wait_ge(scored, 1)
            after(dve.tensor_tensor(T.biased[:, :, :], T.score[:, :, :],
                                    T.ebias[:, :].unsqueeze(1).to_broadcast([P, NS, E0]), ALU.add))
            for i in range(NS):
                dve.max(T.top[:, i, :], T.biased[:, i, :]).then_inc(top_done, 1)
                dve.wait_ge(top_done, i + 1)
                dve.max_index(T.idx[:, i, :], T.top[:, i, :], T.biased[:, i, :]).then_inc(idx_done, 1)
            dve.wait_ge(idx_done, NS)
            after(dve.tensor_copy(T.idx_f[:, :, :], T.idx[:, :, :]))
            for k in range(TOPK):
                dst = T.sel if k == 0 else T.hot
                after(dve.tensor_tensor(dst[:, :, :], T.iota_f[:, :].unsqueeze(1).to_broadcast([P, NS, E0]),
                                        T.idx_f[:, :, k:k + 1].to_broadcast([P, NS, E0]), ALU.is_equal))
                if k:
                    after(dve.tensor_tensor(T.sel[:, :, :], T.sel[:, :, :], T.hot[:, :, :], ALU.add))
            dve.tensor_scalar(T.sel_b[:, :, :], T.sel[:, :, :], T.rowvalid[:, 0:1], None, ALU.mult)\
               .then_inc(chosen, 1)
            after(dve.tensor_tensor(T.gate[:, :, :], T.score[:, :, :], T.sel[:, :, :], ALU.mult))
            after(dve.tensor_reduce(T.wsum[:, :], T.gate[:, :, :], AX.X, ALU.add))
            after(dve.tensor_scalar(T.wsum[:, :], T.wsum[:, :], 1e-12, None, ALU.max))
            after(dve.reciprocal(T.wsum[:, :], T.wsum[:, :]))
            after(dve.tensor_tensor(T.gate[:, :, :], T.gate[:, :, :],
                                    T.wsum[:, :].unsqueeze(2).to_broadcast([P, NS, E0]), ALU.mult))
            dve.wait_ge(counted, 1)
            after(dve.memset(T.before[:, 0, :], 0.0))
            for i in range(1, NS):
                after(dve.tensor_tensor(T.before[:, i, :], T.before[:, i - 1, :],
                                        T.psum[:, 2, E0 * (i - 1):E0 * i], ALU.add))
            after(dve.tensor_tensor(flat(T.before[:, :, :]), flat(T.before[:, :, :]), T.psum[:, 1, :], ALU.add))
            after(dve.tensor_scalar(T.before[:, :, :], T.before[:, :, :], float(CAP), None, ALU.is_lt))
            dve.tensor_tensor(T.gate[:, :, :], T.gate[:, :, :], T.before[:, :, :], ALU.mult).then_inc(gated, 1)


def gates1(nc, ctx, T):
    sem = lambda n: ctx.enter_context(nc.semaphore(f"g1_{n}"))
    logits, shifted, expd, step, gated, turned = (
        sem("logits"), sem("shifted"), sem("expd"), sem("step"), sem("gated"), sem("turned"))
    top_done, idx_done = sem("top"), sem("idx")
    lg = T.score[:, :, 0:E1]
    with nc.Block() as block:

        @block.tensor
        def _(pe):
            for i in range(NS):
                ins = pe.matmul(T.psum[:, 0, E1 * i:E1 * i + E1], T.xT[:, i, :], T.wr[:, :], start=True, stop=True)
            ins.then_inc(logits, 1)
            pe.wait_ge(gated, 1)
            for i in range(NS):
                ins = pe.transpose(T.psum[0:E1, 4 + i // 4, P * (i % 4):P * (i % 4) + P], T.gate[:, i, 0:E1],
                                   T.ident[:, :])
            ins.then_inc(turned, 1)

        @block.scalar
        def _(act):
            act.wait_ge(shifted, 1)
            act.activation(T.biased[:, :, 0:E1], lg, ACT.Exp).then_inc(expd, 1)
            act.wait_ge(turned, 1)
            for b in range(4):
                act.activation(T.gateT[0:E1, P * 4 * b:P * 4 * b + 4 * P], T.psum[0:E1, 4 + b, :], ACT.Copy)

        @block.vector
        def _(dve):
            n = [0]

            def after(ins):
                ins.then_inc(step, 1)
                n[0] += 1
                dve.wait_ge(step, n[0])

            dve.wait_ge(logits, 1)
            after(dve.tensor_tensor(lg, T.psum[:, 0, 0:NS * E1].rearrange("p (i e) -> p i e", e=E1),
                                    T.br[:, :].unsqueeze(1).to_broadcast([P, NS, E1]), ALU.add))
            after(dve.tensor_reduce(T.wsum[:, :], lg, AX.X, ALU.max))
            dve.tensor_tensor(lg, lg, T.wsum[:, :].unsqueeze(2).to_broadcast([P, NS, E1]), ALU.subtract)\
               .then_inc(shifted, 1)
            dve.wait_ge(expd, 1)
            for i in range(NS):
                dve.max(T.top[:, i, :], T.biased[:, i, 0:E1]).then_inc(top_done, 1)
                dve.wait_ge(top_done, i + 1)
                dve.max_index(T.idx[:, i, :], T.top[:, i, :], T.biased[:, i, 0:E1]).then_inc(idx_done, 1)
            dve.wait_ge(idx_done, NS)
            after(dve.tensor_copy(T.idx_f[:, :, :], T.idx[:, :, :]))
            after(dve.tensor_reduce(T.wsum[:, :], T.biased[:, :, 0:E1], AX.X, ALU.add))
            after(dve.reciprocal(T.wsum[:, :], T.wsum[:, :]))
            after(dve.tensor_tensor(T.wsum[:, :], T.wsum[:, :], T.top[:, :, 0], ALU.mult))
            after(dve.tensor_tensor(T.hot[:, :, 0:E1], T.iota_f[:, 0:E1].unsqueeze(1).to_broadcast([P, NS, E1]),
                                    T.idx_f[:, :, 0:1].to_broadcast([P, NS, E1]), ALU.is_equal))
            dve.tensor_tensor(T.gate[:, :, 0:E1], T.hot[:, :, 0:E1],
                              T.wsum[:, :].unsqueeze(2).to_broadcast([P, NS, E1]), ALU.mult).then_inc(gated, 1)


def experts(nc, ctx, T, layer):
    sem = lambda n: ctx.enter_context(nc.semaphore(f"e{layer}_{n}"))
    staged, up_ready, side_ready, gate_ready = sem("staged"), sem("up_ready"), sem("side_ready"), sem("gate_ready")
    act_done, prod_done, gated, down_done = sem("act_done"), sem("prod_done"), sem("gated"), sem("down_done")
    y_copied, y_turned = sem("y_copied"), sem("y_turned")
    x_added = sem("x_added")
    units = 17 if layer == 0 else 16
    per = 3 if layer == 0 else 2
    chunk = lambda t, c, rows=P: t[0:rows, 4 * c:4 * c + 4, :].rearrange("p i (b q) -> p (i b) q", b=2)[:, :, 0:S]
    gateT = T.gateT[:, :].rearrange("p (i q) -> p i q", q=P)
    N = 8 * S
    W1, W3, W2, PK = T.stage

    def run(eng, unit):
        unit(0, 0)
        with eng.Fori(0, 7) as k:
            unit(2 * k + 1, 1)
            unit(2 * k + 2, 0)
        for u in range(15, units):
            unit(u, u % 2)

    with nc.Block() as block:

        @block.tensor
        def _(pe):
            def down(u, par, c, first, last):
                m = 4 * u + c
                pe.wait_ge(gated, m + 1)
                pe.matmul(T.psum[:, c, 0:N], W2[par][:, :], T.hid[c % 2][:, :], start=first,
                          stop=last, skip_group_check=True).then_inc(down_done, 1)

            def unit(u, par, first, with_prev):
                pe.wait_ge(staged, u + 1)
                for c in range(TOKC):
                    m = 4 * u + c
                    hb = [T.psum[:, 4 + (per * c + k) % 4, 0:N] for k in range(per)]
                    if layer == 0:
                        above_zero(pe, gated, m - 1)
                        pe.matmul(hb[0], W1[par][:, :], chunk(T.xT, c), start=True, stop=True).then_inc(up_ready, 1)
                        above_zero(pe, act_done, m)
                        pe.matmul(hb[1], W3[par][:, :], chunk(T.xT, c), start=True, stop=True).then_inc(side_ready, 1)
                        above_zero(pe, prod_done, m)
                        pe.matmul(hb[2], PK[par][:, :], chunk(gateT, c), start=True, stop=True).then_inc(gate_ready, 1)
                    else:
                        above_zero(pe, act_done, m - 1)
                        pe.matmul(hb[0], W1[par][:, :], chunk(T.xT, c), start=True, stop=True).then_inc(up_ready, 1)
                        above_zero(pe, gated, m - 1)
                        pe.matmul(hb[1], PK[par][:, :], chunk(gateT, c), start=True, stop=True).then_inc(gate_ready, 1)
                    if c > 0:
                        down(u, par, c - 1, first, False)
                    elif with_prev:
                        down(u - 1, 1 - par, 3, False, False)

            unit(0, 0, True, False)
            down(0, 0, 3, True, False)
            with pe.Fori(0, 7) as k:
                unit(2 * k + 1, 1, False, False)
                unit(2 * k + 2, 0, False, True)
                down(2 * k + 2, 0, 3, False, False)
            for u in range(15, units):
                unit(u, u % 2, False, u > 15)
            down(units - 1, (units - 1) % 2, 3, False, True)
            if layer == 1:
                for c in range(TOKC):
                    ins = pe.matmul(T.psum[:, c, 0:N], T.b2[0:E1, :], chunk(gateT, c, E1), start=False,
                                    stop=True, skip_group_check=True)
                ins.then_inc(down_done, 1)
            pe.wait_ge(y_copied, TOKC)
            for i in range(NS):
                ins = pe.transpose(T.psum[:, 4 + i // 4, P * (i % 4):P * (i % 4) + P], T.xT[:, i, :], T.ident[:, :])
            ins.then_inc(y_turned, 1)

        @block.scalar
        def _(act):
            def unit(u, par):
                for c in range(TOKC):
                    m = 4 * u + c
                    act.wait_ge(up_ready, m + 1)
                    above_zero(act, prod_done if layer == 0 else gated, m - 1)
                    src = T.psum[:, 4 + (per * c) % 4, 0:N]
                    if layer == 0:
                        act.activation(T.acted[c % 2][:, :], src, ACT.Silu).then_inc(act_done, 1)
                    else:
                        act.activation(T.acted[c % 2][:, :], src, ACT.Gelu, bias=T.b1_now[par][:, :]).then_inc(act_done, 1)

            run(act, unit)
            act.wait_ge(down_done, 4 * units + layer)
            for c in range(TOKC):
                act.activation(chunk(T.xT, c), T.psum[:, c, 0:N].rearrange("p (i q) -> p i q", q=S), ACT.Copy)\
                   .then_inc(y_copied, 1)

        @block.vector
        def _(dve):
            def stage(u, par):
                copies = [(W1, T.w1[layer]), (PK, T.pick[layer]), (W2, T.w2[layer])]
                if layer == 0:
                    copies.insert(0, (W3, T.w3))
                else:
                    copies.insert(0, (T.b1_now, T.b1))
                above_zero(dve, down_done, 4 * (u - 1))
                for dst, src in copies:
                    ins = dve.tensor_scalar(dst[par][:, :], src[:, u, :], 1.0, None, ALU.mult)
                ins.then_inc(staged, 1)

            stage(0, 0)

            def unit(u, par):
                for c in range(TOKC):
                    m = 4 * u + c
                    if c == 2 and not (isinstance(u, int) and u == units - 1):
                        stage(u + 1, 1 - par)
                    dve.wait_ge(act_done, m + 1)
                    if layer == 0:
                        dve.wait_ge(side_ready, m + 1)
                        above_zero(dve, gated, m - 1)
                        dve.tensor_tensor(T.prod[c % 2][:, :], T.acted[c % 2][:, :], T.psum[:, 4 + (per * c + 1) % 4, 0:N],
                                          ALU.mult).then_inc(prod_done, 1)
                        dve.wait_ge(prod_done, m + 1)
                    dve.wait_ge(gate_ready, m + 1)
                    above_zero(dve, down_done, m - 1)
                    dve.tensor_tensor(T.hid[c % 2][:, :], T.prod[c % 2][:, :] if layer == 0 else T.acted[c % 2][:, :],
                                      T.psum[:, 4 + (per * c + per - 1) % 4, 0:N], ALU.mult).then_inc(gated, 1)

            run(dve, unit)
            dve.wait_ge(y_turned, 1)
            for b in range(4):
                dve.tensor_tensor(T.x[:, 4 * b:4 * b + 4, :], T.x[:, 4 * b:4 * b + 4, :],
                                  T.psum[:, 4 + b, :].rearrange("p (i d) -> p i d", d=D), ALU.add).then_inc(x_added, 1)


def cross_attention_ffn_kernel(nc, A, out):
    with ExitStack() as ctx:
        def sb(name, shape, dt=F32):
            return ctx.enter_context(nc.sbuf_tensor(name, shape, dt))

        T = Tiles()
        T.psum = ctx.enter_context(nc.psum_tensor("psum", [P, 8, 512], F32))
        T.masked = [-173.0 * 2.0 ** 59, 1e-9]
        T.x = sb("x_rows", [P, NS, D])
        T.xn = sb("xn", [P, NS, D])
        T.xT = sb("xT", [P, NS, P])
        T.qT = T.xn
        T.w_in = sb("w_in", [P, 2, 3, D])
        T.w_t = sb("w_t", [P, 2, 3, D])
        T.bq, T.bk = sb("bq", [P, 2]), sb("bk", [P, 2])
        T.bv, T.bo = sb("bv", [P, 2, D]), sb("bo", [P, 2, D])
        T.wo_in, T.woa, T.wo = sb("wo_in", [P, D]), sb("woa", [P, 4, D]), sb("wo", [P, 2, 4, D])
        T.gw_in, T.gw = sb("gw_in", [E0, D], BF16), sb("gw", [P, E0])
        T.sw1_in, T.sw3_in = sb("sw1_in", [I0, D], BF16), sb("sw3_in", [I0, D], BF16)
        T.sw2_in = sb("sw2_in", [D, I0], BF16)
        T.ebias, T.wr, T.br = sb("ebias", [P, E0]), sb("wr", [P, E1]), sb("br", [P, E1])
        T.b1, T.b2 = sb("b1", [P, 16, 1]), sb("b2", [E1, D])
        T.w1 = [sb("w1_0", [P, 17, P], BF16), sb("w1_1", [P, 16, P])]
        T.w3 = sb("w3", [P, 17, P], BF16)
        T.w2 = [sb("w2_0", [P, 17, D], BF16), sb("w2_1", [P, 16, D])]
        T.pick = [sb("pick_0", [P, 17, P], BF16), sb("pick_1", [P, 16, P], BF16)]
        T.stage = [[sb(f"stage_{n}{k}", [P, P]) for k in range(2)] for n in ("w1", "w3", "w2", "pick")]
        T.b1_now = [sb(f"b1_now{k}", [P, 1]) for k in range(2)]
        T.ident, T.ident_b = sb("ident", [P, P]), sb("ident_b", [P, P], BF16)
        T.headmask, T.densel = sb("headmask", [P, H]), sb("densel", [P, 4, P])
        T.earlier, T.ones_b = sb("earlier", [P, P], BF16), sb("ones_b", [P, P], BF16)
        T.iota_i, T.iota_f, T.rowvalid = sb("iota_i", [P, E0], I32), sb("iota_f", [P, E0]), sb("rowvalid", [P, 1])
        T.idq = sb("idq", [P, S])
        T.hide = sb("hide", [P, 2, SK], BF16)
        T.mkT = sb("mkT", [P, 2, KT, S])
        T.shiftw = sb("shiftw", [P, 2, 2, SK], BF16)
        T.count, T.floor, T.tmp1 = sb("count", [P, 2]), sb("floor", [P, 2]), sb("tmp1", [P, 1])
        T.countbv = sb("countbv", [P, 2, D])
        T.stats, T.moments = sb("stats", [P, NS, 6]), sb("moments", [P, NS, 2])
        T.var, T.std, T.rstd = sb("var", [P, NS]), sb("std", [P, NS]), sb("rstd", [P, NS, 1])
        T.ctx = [sb(f"ctx{k}", [P, KT, D]) for k in range(2)]
        T.mask0 = T.ctx[0][:].rearrange("p t d -> p (t d)")[:, 0:SK].bitcast(I32)
        T.mask1 = T.ctx[1][:].rearrange("p t d -> p (t d)")[:, 0:SK // 4].bitcast(I32)
        T.ctxT = sb("ctxT", [P, SK])
        T.k = [sb(f"k{k}", [P, SK]) for k in range(2)]
        T.mk = T.k[0][:, :].bitcast(BF16).rearrange("p (l k) -> p l k", l=2)
        T.kbf = sb("kbf", [P, SK], BF16)
        T.v = [sb(f"v{k}", [P, KT, VCOLS]) for k in range(2)]
        T.probs = [sb(f"probs{k}", [P, H * S]) for k in range(3)]
        T.qblk = [sb(f"qblk{k}", [P, H, S]) for k in range(2)]
        T.qbf = sb("qbf", [P, HP, 2, HALF], BF16)
        T.mvr = [sb(f"shift_rows{k}", [P, 2, HP, S], BF16) for k in range(2)]
        T.de = [sb(f"masked_weights{k}", [P, H, S]) for k in range(2)]
        T.mv9 = [sb(f"masked_values{k}", [P, VCOLS]) for k in range(2)]
        T.gt = sb("masked_ctx", [P, P])
        T.junk = sb("junk", [P, SK], BF16)
        T.rowmax, T.negm, T.emask = sb("rowmax", [P, HP]), sb("negm", [P, HP], BF16), sb("emask", [P, HP])
        T.earg = sb("earg", [P, HP])
        T.sums, T.recip, T.attn = sb("sums", [P, 4 * S]), sb("recip", [P, 4 * S]), sb("attn", [P, 4 * S])
        T.gateT = sb("gateT", [P, NS * P])
        flat_k = [T.k[j] for j in range(2)]
        T.sel = T.probs[0][:, 0:512].rearrange("p (i e) -> p i e", e=E0)
        T.hot = T.probs[1][:, 0:512].rearrange("p (i e) -> p i e", e=E0)
        T.gate = T.probs[2][:, 0:512].rearrange("p (i e) -> p i e", e=E0)
        T.score = flat_k[0][:, 0:512].rearrange("p (i e) -> p i e", e=E0)
        T.biased = flat_k[0][:, 512:1024].rearrange("p (i e) -> p i e", e=E0)
        T.before = flat_k[1][:, 0:512].rearrange("p (i e) -> p i e", e=E0)
        T.sel_b = sb("sel_b", [P, NS, E0], BF16)
        T.top, T.idx, T.idx_f = sb("top", [P, NS, 8]), sb("idx", [P, NS, 8], U32), sb("idx_f", [P, NS, 8])
        T.wsum = sb("wsum", [P, NS])
        N = 8 * S
        T.acted = [T.ctxT[:, N * k:N * k + N] for k in range(2)]
        T.prod = [T.ctxT[:, 2 * N:3 * N], flat_k[0][:, 0:N]]
        T.hid = [flat_k[1][:, 512:512 + N], flat_k[1][:, 512 + N:512 + 2 * N]]
        T.carrier, T.turn = sb("carrier", [P, 1]), sb("turn", [P, 1])

        constants_and_loads(nc, ctx, A, T)
        prepare(nc, ctx, A, T)
        normalise(nc, ctx, T, "n0")
        queries(nc, ctx, T, 0)
        attention(nc, ctx, A, T, 0)
        normalise(nc, ctx, T, "n1")
        gates0(nc, ctx, T)
        experts(nc, ctx, T, 0)
        normalise(nc, ctx, T, "n2")
        queries(nc, ctx, T, 1)
        attention(nc, ctx, A, T, 1)
        normalise(nc, ctx, T, "n3")
        gates1(nc, ctx, T)
        experts(nc, ctx, T, 1)

        stored = ctx.enter_context(nc.semaphore("stored"))
        with nc.Block() as block:

            @block.sync
            def _(sp):
                for par in range(2):
                    sp.dma_start(out.rearrange("(i two) q d -> two q i d", two=2)[par],
                                 T.x[HALF * par:HALF * par + S, :, :]).then_inc(stored, 16)
                sp.wait_ge(stored, 32)


_INS = ['x', 'ctx_1024', 'mask_1x1xSxS2_ik0', 'mask_1x1xSxS2_bk0'] + \
       [f'L{j}_xattn_{w}' for j in range(2) for w in ('Wq', 'bq', 'Wk', 'bk', 'Wv', 'bv', 'Wo', 'bo')] + \
       [f'L0_ffn_{w}' for w in ('gate_w', 'bias', 'W1', 'W3', 'W2', 'sw1', 'sw3', 'sw2')] + \
       [f'L1_ffn_{w}' for w in ('Wr', 'br', 'W1', 'b1', 'W2', 'b2')]


def kernel(**inputs):
    import numpy as _np
    import concourse.bacc as _bacc
    from concourse import mybir as _mybir
    from concourse.bass_utils import run_bass_kernel_spmd as _run

    nc = _bacc.Bacc("TRN2", target_bir_lowering=False, num_devices=1)
    arrays, aps = {}, {}
    for name in _INS:
        a = _np.ascontiguousarray(inputs[name])
        if a.dtype == _np.bool_:
            a = a.view(_np.int32)
        arrays[f"in_{name}"] = a
        aps[name] = nc.dram_tensor(f"in_{name}", a.shape, _mybir.dt.from_np(a.dtype), kind="ExternalInput").ap()
    out = nc.dram_tensor("out_x", (NB, S, D), F32, kind="ExternalOutput").ap()
    cross_attention_ffn_kernel(nc, aps, out)
    r = _run(nc, [arrays], core_ids=[0])
    return r.results[0]["out_x"]
```

```python
from contextlib import ExitStack

import concourse.bass as bass
from concourse import mybir

ALU = mybir.AluOpType
ACT = mybir.ActivationFunctionType
AX = mybir.AxisListType
F32 = mybir.dt.float32
BF16 = mybir.dt.bfloat16
I32 = mybir.dt.int32
U32 = mybir.dt.uint32
U8 = mybir.dt.uint8

P = 128
NB = 32
S = 56
D = 128
H = 16
DH = D // H
SK = 1500
KT = 12
KP = SK // KT
HALF = 64
NS = NB // 2
HP = H // 2
HQ = HP * S
VW = DH + 1
VCOLS = 168
CHUNK = 4 * KP
SCALE = 1.0 / float(DH) ** 0.5
EPS = 1e-5
HIDE = -1e30
NONE = -3e38
NG, GR = 4, 32
K_PART = (0, 1, 2, 0)
STACKED = 16 * NG * len(K_PART)
E0, I0, TOPK, CAP = 32, 64, 4, 2 * 512 * 4 // 32
E1, F1 = 8, 256
TOKC = 4


class Tiles:
    pass


def above_zero(eng, sem, value):
    if isinstance(value, int) and value <= 0:
        return
    eng.wait_ge(sem, value)


def wait_apart(dve, T, sem, value, column=0):
    above_zero(dve, sem, value)
    dve.memset(T.carrier[:, column:column + 1], 0.0)


def constants_and_loads(nc, ctx, A, T):
    sem = lambda n: ctx.enter_context(nc.semaphore(n))
    zeroed, loaded, made = sem("tiles_zeroed"), sem("inputs_loaded"), sem("constants_made")
    T.n_loads = 0
    with nc.Block() as block:

        @block.sync
        def _(sp):
            def load(dst, src):
                sp.dma_start(dst, src).then_inc(loaded, 16)
                T.n_loads += 1

            for j in range(2):
                load(T.w_in[:, j, 0], A[f"L{j}_xattn_Wq"])
                load(T.w_in[:, j, 1], A[f"L{j}_xattn_Wk"])
                load(T.w_in[:, j, 2], A[f"L{j}_xattn_Wv"])
                load(T.bq[:, j:j + 1], A[f"L{j}_xattn_bq"].rearrange("(n a) -> n a", a=1))
                load(T.bk[:, j:j + 1], A[f"L{j}_xattn_bk"].rearrange("(n a) -> n a", a=1))
                load(T.bv[:, j], A[f"L{j}_xattn_bv"].partition_broadcast(P))
                load(T.bo[:, j], A[f"L{j}_xattn_bo"].partition_broadcast(P))
            load(T.wo_in[:, :], A["L1_xattn_Wo"])
            load(T.gw_in[:, :], A["L0_ffn_gate_w"])
            load(T.sw1_in[:, :], A["L0_ffn_sw1"])
            load(T.sw3_in[:, :], A["L0_ffn_sw3"])
            load(T.sw2_in[:, :], A["L0_ffn_sw2"])
            load(T.ebias[:, :], A["L0_ffn_bias"].partition_broadcast(P))
            load(T.wr[:, :], A["L1_ffn_Wr"])
            load(T.br[:, :], A["L1_ffn_br"].partition_broadcast(P))
            load(T.b2[:, :], A["L1_ffn_b2"])
            sp.wait_ge(zeroed, 8)
            for par in range(2):
                rows = slice(HALF * par, HALF * par + S)
                load(T.x[rows, :, :], A["x"].rearrange("(i two) q d -> two q i d", two=2)[par])
                load(T.mask0[rows, :], A["mask_1x1xSxS2_ik0"][0, 0])
                load(T.mask1[rows, :], A["mask_1x1xSxS2_bk0"][0, 0])
            wo = A["L0_xattn_Wo"]
            for g in range(4):
                for j in range(4):
                    h = 3 * g + j if j < 3 else 12 + g
                    r = 32 * g + (VW * j if j < 3 else 0)
                    load(T.wo[r:r + DH, 0, j, :], wo[DH * h:DH * h + DH, :])
            with nc.allow_non_contiguous_dma(reason="expert weights, once"):
                load(T.w1[0][:, 0:16, :].rearrange("p u (j i) -> p (u j) i", j=2),
                     A["L0_ffn_W1"].rearrange("e d i -> d e i"))
                load(T.w3[:, 0:16, :].rearrange("p u (j i) -> p (u j) i", j=2),
                     A["L0_ffn_W3"].rearrange("e d i -> d e i"))
                load(T.w2[0][:, 0:16, :], A["L0_ffn_W2"].rearrange("(u j) i d -> (j i) u d", j=2))
                load(T.b1[:, :, 0], A["L1_ffn_b1"].rearrange("e (a f) -> f (e a)", a=2))
            sp.wait_ge(loaded, 16 * T.n_loads)

        @block.vector
        def _(dve):
            for tile, value in ((T.x, 0.0), (T.mask0, 1), (T.mask1, 0), (T.wo, 0.0), (T.w1[0], 0.0),
                                (T.w3, 0.0), (T.w2[0], 0.0), (T.mv9[0], 0.0)):
                dve.memset(tile[:], value).then_inc(zeroed, 1)
            for tile in (T.v[0], T.v[1], T.mv9[1], T.gt, T.mvr[0], T.mvr[1],
                         T.de[0], T.de[1], T.qbf, T.woa):
                dve.memset(tile[:], 0.0).then_inc(zeroed, 1)
            dve.memset(T.ones_b[:], 1.0)
            dve.wait_ge(zeroed, 18)
            for v in T.v:
                dve.memset(v[:, :, 0:H * VW].rearrange("p t (h d) -> p t h d", d=VW)[:, :, :, DH:VW], 1.0)

        @block.gpsimd
        def _(pool):
            n = [0]

            def made_by(ins):
                ins.then_inc(made, 1)
                n[0] += 1
                pool.wait_ge(made, n[0])

            def one_where_zero(tile, base, pattern, mult=1):
                made_by(pool.memset(tile, 0.0))
                made_by(pool.affine_select(out=tile, in_=tile, compare_op=ALU.not_equal, fill=1.0,
                                           base=base, pattern=pattern, channel_multiplier=mult))

            one_where_zero(T.ident[:, :], 0, [[-1, P]])
            one_where_zero(T.ident_b[:, :], 0, [[-1, P]])
            made_by(pool.memset(T.headmask[:, :], 1.0))
            made_by(pool.affine_select(out=T.headmask[:, :], in_=T.headmask[:, :], compare_op=ALU.is_ge,
                                       fill=0.0, base=0, pattern=[[-DH, H]], channel_multiplier=1))
            made_by(pool.affine_select(out=T.headmask[:, :], in_=T.headmask[:, :], compare_op=ALU.is_ge,
                                       fill=0.0, base=DH - 1, pattern=[[DH, H]], channel_multiplier=-1))
            for j in range(4):
                first = VW * j + DH if j < 3 else DH
                one_where_zero(T.densel[:, j, :], -first, [[-32, 4], [0, 32]])
            one_where_zero(T.stackq[:, :, :], 0, [[-GR, NG], [0, NG], [-1, GR]])
            made_by(pool.memset(T.qb[0][:, :, :, :], 0.0))
            made_by(pool.memset(T.qb[1][:, :, :, :], 0.0))
            for tile, pattern in ((T.pick[0], [[-2, 16], [-1, 2], [0, 64]]), (T.pick[1], [[-1, 8], [0, 2], [0, P]])):
                made_by(pool.memset(tile[:, :, :], 0.0))
                for r in range(3):
                    made_by(pool.affine_select(out=tile[:, :, :], in_=tile[:, :, :], compare_op=ALU.not_equal,
                                               fill=1.0, base=-E0 * r, pattern=pattern, channel_multiplier=1))
            made_by(pool.memset(T.earlier[:, :], 1.0))
            made_by(pool.affine_select(out=T.earlier[:, :], in_=T.earlier[:, :], compare_op=ALU.is_gt,
                                       fill=0.0, base=0, pattern=[[1, P]], channel_multiplier=-1))
            made_by(pool.iota(T.iota_i[:, :], pattern=[[1, E0]], base=0, channel_multiplier=0))
            made_by(pool.tensor_copy(T.iota_f[:, :], T.iota_i[:, :]))
            made_by(pool.memset(T.turn[:, :], 0.0))
            made_by(pool.memset(T.rowvalid[:, :], 0.0))
            for par in range(2):
                pool.memset(T.idq[:, :], 0.0) if par == 0 else None
                made_by(pool.memset(T.rowvalid[HALF * par:HALF * par + S, :], 1.0))
            made_by(pool.tensor_tensor(T.idq[:, :], T.ident[:, 0:S], T.ident[:, HALF:HALF + S], ALU.add))


def prepare(nc, ctx, A, T):
    sem = lambda n: ctx.enter_context(nc.semaphore(n))
    turned, masks_made, step = sem("weights_turned"), sem("masks_made"), sem("prepare_step")
    big = [T.psum[:, b, :] for b in range(8)]
    with nc.Block() as block:

        @block.tensor
        def _(pe):
            for k in range(3):
                pe.transpose(big[0][:, P * k:P * k + P], T.w_in[:, 1, k], T.ident[:, :])
            pe.matmul(big[2][:, 0:E0], T.gw_in[:, :], T.ident_b[0:E0, 0:E0], start=True, stop=True)
            pe.matmul(big[2][:, 64:64 + I0], T.sw1_in[:, :], T.ident_b[0:I0, 0:I0], start=True, stop=True)
            pe.matmul(big[2][:, 128:128 + I0], T.sw3_in[:, :], T.ident_b[0:I0, 0:I0], start=True, stop=True)
            pe.matmul(big[3][0:I0, 0:D], T.sw2_in[:, :], T.ident_b[:, :], start=True, stop=True)
            pe.wait_ge(masks_made, 1)
            for j in range(4):
                pe.transpose(big[1][:, P * j:P * j + P], T.woa[:, j, :], T.ident[:, :])
            pe.wait_ge(masks_made, 3)
            for layer in range(2):
                for t in range(KT):
                    ins = pe.matmul(big[4 + 2 * layer + t // 6][0:KP, S * (t % 6):S * (t % 6) + S],
                                    T.mk[0:S, layer, KP * t:KP * t + KP], T.ident_b[0:S, 0:S],
                                    start=True, stop=True)
            ins.then_inc(turned, 1)

        @block.vector
        def _(dve):
            n = [0]

            def after(ins):
                ins.then_inc(step, 1)
                n[0] += 1
                dve.wait_ge(step, n[0])

            for j in range(4):
                src = T.wo_in[:, 0:96] if j < 3 else T.wo_in[:, 96:128]
                if j < 3:
                    src = src.rearrange("p (g k d) -> p g k d", g=4, k=3)[:, :, j, :]
                else:
                    src = src.rearrange("p (g d) -> p g d", g=4)
                off = VW * j if j < 3 else 0
                dst = T.woa[:, j, :].rearrange("p (g r) -> p g r", g=4)[:, :, off:off + DH]
                ins = dve.tensor_copy(dst, src)
            ins.then_inc(masks_made, 1)
            for layer in range(2):
                src = (T.mask0 if layer == 0 else T.mask1.bitcast(U8))[:, :].rearrange("q (p t) -> q t p", t=KT)
                dst = T.mk[:, layer, :].rearrange("q (t p) -> q t p", t=KT)
                dve.tensor_scalar(dst, src, 0.0, None, ALU.is_equal if layer == 0 else ALU.not_equal)\
                   .then_inc(masks_made, 1)
            dve.wait_ge(masks_made, 3)
            for layer in range(2):
                masked = T.mk[:, layer, :]
                after(dve.tensor_scalar(T.hide[:, layer, :], masked, HIDE, None, ALU.mult))
                after(dve.tensor_reduce(T.count[:, layer:layer + 1], masked, AX.X, ALU.add))
                after(dve.tensor_reduce(T.floor[:, layer:layer + 1], masked, AX.X, ALU.max))
                after(dve.tensor_scalar(T.tmp1[:, :], T.floor[:, layer:layer + 1], -1.0, -NONE,
                                        ALU.add, ALU.mult))
                after(dve.scalar_tensor_tensor(out=T.floor[:, layer:layer + 1],
                                               in0=T.floor[:, layer:layer + 1], scalar=T.masked[layer],
                                               in1=T.tmp1[:, :], op0=ALU.mult, op1=ALU.add))
                after(dve.tensor_scalar(T.countbv[:, layer, :], T.bv[:, layer, :],
                                        T.count[:, layer:layer + 1], None, ALU.mult))
                after(dve.tensor_scalar(T.bq[:, layer:layer + 1], T.bq[:, layer:layer + 1], SCALE, None, ALU.mult))
                after(dve.memset(T.shiftw[:, layer, :, :], 1.0))
                dve.tensor_copy(T.shiftw[HALF:P, layer, 0, :], T.hide[HALF:P, layer, :])
                after(dve.tensor_copy(T.shiftw[0:HALF, layer, 1, :], T.hide[0:HALF, layer, :]))
            after(dve.tensor_reduce(T.groupmask[:, :], T.headmask[:, :].rearrange("p (k a) -> p a k", a=NG),
                                    AX.X, ALU.add))
            for par in range(2):
                for p in range(HP):
                    dve.tensor_copy(T.mvr[par][HALF:HALF + S, 0, p, :], T.idq[HALF:HALF + S, :])
                    after(dve.tensor_copy(T.mvr[par][0:S, 1, p, :], T.idq[0:S, :]))
            dve.wait_ge(turned, 1)
            after(dve.tensor_copy(T.w_t[:, 1].rearrange("p k n -> p (k n)"), big[0][:, 0:3 * P]))
            after(dve.tensor_copy(T.w_t[:, 0], T.w_in[:, 0]))
            after(dve.tensor_copy(T.wo[:, 1].rearrange("p j n -> p (j n)"), big[1][:, :]))
            after(dve.tensor_copy(T.gw[:, :], big[2][:, 0:E0]))
            after(dve.tensor_copy(T.w1[0][:, 16, 0:I0], big[2][:, 64:64 + I0]))
            after(dve.tensor_copy(T.w3[:, 16, 0:I0], big[2][:, 128:128 + I0]))
            after(dve.tensor_copy(T.w2[0][0:I0, 16, :], big[3][0:I0, 0:D]))
            for layer in range(2):
                for half in range(2):
                    after(dve.tensor_copy(
                        T.mkT[0:KP, layer, 6 * half:6 * half + 6, :],
                        big[4 + 2 * layer + half][0:KP, 0:6 * S].rearrange("p (t q) -> p t q", t=6)))


def normalise(nc, ctx, T, name, weights=None):
    sem = lambda n: ctx.enter_context(nc.semaphore(f"{name}_{n}"))
    stats_done, moments_done, std_done, xn_done = sem("stats"), sem("moments"), sem("std"), sem("xn")
    step, turned, copied = sem("step"), sem("turned"), sem("copied")
    loaded = None if weights is None else sem("loaded")
    with nc.Block() as block:

        @block.sync
        def _(sp):
            if weights is not None:
                sp.dma_start(T.w1[1][:, :, :].rearrange("p (e a) f -> p e (a f)", a=2),
                             weights[0].rearrange("e d f -> d e f")).then_inc(loaded, 16)
                for a in range(2):
                    sp.dma_start(T.w2[1][:, :, :].rearrange("p (e a) d -> p e a d", a=2)[:, :, a],
                                 weights[1].rearrange("e (a f) d -> a f e d", a=2)[a]).then_inc(loaded, 16)
                sp.wait_ge(loaded, 48)

        @block.vector
        def _(dve):
            for i in range(NS):
                dve.bn_stats(T.stats[:, i, :], T.x[:, i, :]).then_inc(stats_done, 1)
                dve.wait_ge(stats_done, i + 1)
                dve.bn_aggr(T.moments[:, i, :], T.stats[:, i, :]).then_inc(moments_done, 1)
            dve.wait_ge(moments_done, NS)
            dve.tensor_scalar(T.var[:, :], T.moments[:, :, 1], EPS, None, ALU.add).then_inc(step, 1)
            dve.wait_ge(std_done, 1)
            dve.reciprocal(T.rstd[:, :, 0], T.std[:, :]).then_inc(step, 1)
            dve.wait_ge(step, 2)
            with dve.Fori(0, NS) as i:
                dve.tensor_scalar(T.xn[:, i, :], T.x[:, i, :], T.moments[:, i, 0:1], T.rstd[:, i, :],
                                  ALU.subtract, ALU.mult).then_inc(xn_done, 1)

        @block.scalar
        def _(act):
            act.wait_ge(step, 1)
            act.activation(T.std[:, :], T.var[:, :], ACT.Sqrt).then_inc(std_done, 1)
            for b in range(4):
                act.wait_ge(turned, b + 1)
                act.activation(T.xT[:, 4 * b:4 * b + 4, :].rearrange("p i t -> p (i t)"),
                               T.psum[:, b, :], ACT.Copy).then_inc(copied, 1)

        @block.tensor
        def _(pe):
            for i in range(NS):
                pe.wait_ge(xn_done, i + 1)
                ins = pe.transpose(T.psum[:, i // 4, P * (i % 4):P * (i % 4) + P], T.xn[:, i, :], T.ident[:, :])
                if i % 4 == 3:
                    ins.then_inc(turned, 1)


def queries(nc, ctx, T, layer):
    sem = lambda n: ctx.enter_context(nc.semaphore(f"q{layer}_{n}"))
    projected, done = sem("projected"), sem("done")
    with nc.Block() as block:

        @block.tensor
        def _(pe):
            for b in range(4):
                pe.matmul(T.psum[:, b, :], T.w_t[:, layer, 0], T.xT[:, 4 * b:4 * b + 4, :].rearrange("p i t -> p (i t)"),
                          start=True, stop=True).then_inc(projected, 1)

        @block.scalar
        def _(act):
            for b in range(4):
                act.wait_ge(projected, b + 1)
                act.activation(T.qT[:, 4 * b:4 * b + 4, :].rearrange("p i t -> p (i t)"), T.psum[:, b, :],
                               ACT.Identity, bias=T.bq[:, layer:layer + 1], scale=SCALE).then_inc(done, 1)

        @block.vector
        def _(dve):
            dve.tensor_tensor(T.x[:, :, :], T.x[:, :, :],
                              T.bo[:, layer, :].unsqueeze(1).to_broadcast([P, NS, D]), ALU.add).then_inc(done, 1)


def attention(nc, ctx, A, T, layer):
    sem = lambda n: ctx.enter_context(nc.semaphore(f"a{layer}_{n}"))
    ctx_landed = [sem("ctx_landed0"), sem("ctx_landed1")]
    ctxT_ready, ctxT_copied = sem("ctxT_ready"), sem("ctxT_copied")
    stacked = sem("stacked")
    split, step_split = sem("split"), sem("step_split")
    qs_up, qs_parts, qs_taken, qs_ready = sem("qs_up"), sem("qs_parts"), sem("qs_taken"), sem("qs_ready")
    k_ready, k_copied = sem("k_ready"), sem("k_copied")
    v_ready, v_copied = sem("v_ready"), sem("v_copied")
    g_ready, g_copied, mv_ready, mv_copied = sem("g_ready"), sem("g_copied"), sem("mv_ready"), sem("mv_copied")
    q_ready = sem("q_ready")
    first_ready, max_taken, max_joined = sem("first_ready"), sem("max_taken"), sem("max_joined")
    negm_ready, earg_ready, shift_ready, emask_ready, de_ready = sem("negm_ready"), sem("earg_ready"), sem("shift_ready"), sem("emask_ready"), sem("de_ready")
    scores_ready, probs_ready, probs_used = sem("scores_ready"), sem("probs_ready"), sem("probs_used")
    sums_ready, sums_copied, den_ready, recip_ready = sem("sums_ready"), sem("sums_copied"), sem("den_ready"), sem("recip_ready")
    attn_ready, out_ready, x_added = sem("attn_ready"), sem("out_ready"), sem("x_added")
    ctx_dram = A["ctx_1024"].rearrange("b (p t) d -> b p t d", t=KT)
    bank = [T.psum[:, j, :] for j in range(3)]
    scores_ps = [T.psum[:, 3:5, 0:HQ], T.psum[:, 5:7, 0:HQ]]
    sums_ps = T.psum[:, 7, 0:4 * S]
    wk, wv = T.w_t[:, layer, 1], T.w_t[:, layer, 2]

    def steps(eng, step):
        step(0, 0, True, False)
        step(0, 1, False, False)
        with eng.Fori(1, NS - 1) as i:
            step(i, 0, False, False)
            step(i, 1, False, False)
        step(NS - 1, 0, False, False)
        step(NS - 1, 1, False, True)

    def after(i, par):
        return (i, 1) if par == 0 else (i + 1, 0)

    with nc.Block() as block:

        @block.sync
        def _(sp):
            for b in range(2):
                sp.dma_start(T.ctx[b][0:KP], ctx_dram[b]).then_inc(ctx_landed[b], 16)

            two_ahead = ctx_dram[2:NB]

            def stack(n, par):
                sp.wait_ge(split, 3 * n + 3)
                for g in range(NG):
                    for r, part in enumerate(K_PART):
                        sp.dma_start(T.ks[GR * r:GR * r + GR, par, g, :], T.kpart[part][GR * g:GR * g + GR, :])\
                          .then_inc(stacked, 16)

            def step(i, par, first, last):
                b = 2 * i + par
                if not (isinstance(i, int) and i == NS - 1):
                    sp.wait_ge(g_ready, b + 1)
                    sp.dma_start(T.ctx[par][0:KP], two_ahead[b]).then_inc(ctx_landed[par], 16)
                if not last:
                    stack(b + 1, 1 - par)

            stack(0, 0)
            steps(sp, step)

        @block.tensor
        def _(pe):
            def turn(i, par, j, to):
                if j == 0:
                    pe.wait_ge(ctx_landed[par], 16 * i + 16)
                for u in range(4):
                    ins = pe.transpose(bank[to][:, KP * u:KP * u + KP], T.ctx[par][0:KP, 4 * j + u, :],
                                       T.ident[0:KP, 0:KP])
                ins.then_inc(ctxT_ready, 1)

            def keys(n, j, to):
                pe.wait_ge(ctxT_copied, 3 * n + j + 1)
                pe.matmul(bank[to][:, 0:CHUNK], wk, T.ctxT[:, CHUNK * j:CHUNK * j + CHUNK],
                          start=True, stop=True).then_inc(k_ready, 1)

            def values(j, to):
                for u in range(4):
                    t = 4 * j + u
                    ins = pe.matmul(bank[to][0:KP, P * u:P * u + P], T.ctxT[:, KP * t:KP * t + KP], wv,
                                    start=True, stop=True)
                ins.then_inc(v_ready, 1)

            def masked_context(par, to):
                for t in range(KT):
                    ins = pe.matmul(bank[to][:, 0:S], T.ctx[par][0:KP, t, :], T.mkT[0:KP, layer, t, :],
                                    start=(t == 0), stop=(t == KT - 1))
                ins.then_inc(g_ready, 1)

            def masked_values(n, to):
                pe.wait_ge(g_copied, n + 1)
                pe.matmul(bank[to][:, 0:D], T.gt[:, :], wv, start=True, stop=True).then_inc(mv_ready, 1)

            def stack_queries(i, par, to):
                for g in range(NG):
                    ins = pe.matmul(bank[to][:, S * g:S * g + S],
                                    T.stackq[:, g, :],
                                    T.qT[:, i, HALF * par:HALF * par + S], start=True, stop=True)
                ins.then_inc(qs_up, 1)

            def first_pass(n, p):
                if p == 0:
                    pe.wait_ge(k_copied, 3 * n + 3)
                    pe.wait_ge(q_ready, n + 1)
                for j in range(3):
                    if p > 0:
                        pe.wait_ge(max_taken, 3 * (HP * n + p - 1) + j + 1)
                    pe.matmul(T.psum[:, j, 0:CHUNK], T.qbf[:, p].rearrange("k a q -> k (a q)"),
                              T.kpart[0][:, CHUNK * j:CHUNK * j + CHUNK], start=True, stop=True)\
                      .then_inc(first_ready, 1)

            def prepare_next(n, i, par, t, late):
                if t == 0 and not late:
                    turn(i, par, 0, 1)
                    turn(i, par, 1, 2)
                if t == 1 and not late:
                    keys(n, 0, 1)
                    keys(n, 1, 2)
                    above_zero(pe, recip_ready, n - 1)
                    turn(i, par, 2, 0)
                if t == 2 and late:
                    pe.wait_ge(ctxT_copied, 3 * n + 3)
                    pe.wait_ge(k_copied, 3 * n + 1)
                    keys(n, 2, 1)
                    pe.wait_ge(k_copied, 3 * n + 2)
                    values(0, 2)
                if t == 3 and not late:
                    above_zero(pe, x_added, n - 1)
                    values(1, 0)
                    pe.wait_ge(k_copied, 3 * n + 3)
                    values(2, 1)
                if t == 3 and late:
                    pe.wait_ge(v_copied, 3 * n + 1)
                    masked_context(par, 2)
                if t == 4 and not late:
                    pe.wait_ge(v_copied, 3 * n + 2)
                    masked_values(n, 0)
                    pe.wait_ge(v_copied, 3 * n + 3)
                    stack_queries(i, par, 1)
                if t == 5 and not late:
                    pe.wait_ge(qs_taken, n + 1)
                    pe.wait_ge(mv_copied, n + 1)
                if t >= 5 and not late:
                    first_pass(n, t - 5)
                if t == KT - 1 and late:
                    first_pass(n, HP - 1)

            def scores(b, i, par, t):
                if t == 0:
                    pe.wait_ge(stacked, STACKED * (b + 1))
                    pe.wait_ge(qs_ready, 2 * (b + 1))
                m = KT * b + t
                above_zero(pe, probs_ready, m - 1)
                for a in range(2):
                    for g in (2 * a, 2 * a + 1):
                        dst = scores_ps[t % 2][0:KP, a, 4 * S * (g % 2):4 * S * (g % 2) + 4 * S]
                        k = T.ks[:, par, g, KP * t:KP * t + KP]
                        pe.matmul(dst, k, T.qa[par][:, g].rearrange("r h q -> r (h q)"), start=(g % 2 == 0),
                                  stop=False, skip_group_check=True)
                        pe.matmul(dst, k, T.qb[par][:, g].rearrange("r h q -> r (h q)"), start=False,
                                  stop=False, skip_group_check=True)

            def shift(b, par, t):
                if t == 0:
                    pe.wait_ge(shift_ready, 2 * (b + 1))
                for a in range(2):
                    ins = pe.matmul(scores_ps[t % 2][0:KP, a, :], T.shiftw[:, layer, a, KP * t:KP * t + KP],
                                    T.mvr[par][:, a].rearrange("r p q -> r (p q)"), start=False, stop=True,
                                    skip_group_check=True)
                ins.then_inc(scores_ready, 1)

            def weigh(values_of, weights, start, stop):
                for g in range(4):
                    pe.matmul(sums_ps[32 * g:32 * g + 32, 0:3 * S], values_of(3 * VW * g),
                              weights[:, 3 * S * g:3 * S * g + 3 * S], start=start, stop=stop,
                              skip_group_check=True)
                for g in range(4):
                    ins = pe.matmul(sums_ps[32 * g:32 * g + 32, 3 * S:4 * S], values_of(12 * VW + VW * g),
                                    weights[:, S * (12 + g):S * (12 + g) + S], start=False, stop=stop,
                                    skip_group_check=True)
                return ins

            def weigh_tile(b, par, t):
                pe.wait_ge(probs_ready, KT * b + t + 1)
                if t == 0:
                    above_zero(pe, sums_copied, b)
                weigh(lambda c: T.v[par][0:KP, t, c:c + 32], T.probs[t % 3][0:KP, :], t == 0, False)\
                    .then_inc(probs_used, 1)

            def weigh_masked(b, par):
                pe.wait_ge(de_ready, 2 * (b + 1))
                weigh(lambda c: T.mv9[par][:, c:c + 32], T.de[par][:, :, :].rearrange("r h q -> r (h q)"),
                      False, True).then_inc(sums_ready, 1)

            def denominators(b):
                pe.wait_ge(sums_copied, b + 1)
                for j in range(4):
                    ins = pe.matmul(bank[0][:, S * j:S * j + S], T.densel[:, j, :], T.sums[:, S * j:S * j + S],
                                    start=True, stop=True)
                ins.then_inc(den_ready, 1)

            def project(b, i, par):
                pe.wait_ge(attn_ready, b + 1)
                rows = slice(HALF * par, HALF * par + S)
                for j in range(4):
                    ins = pe.matmul(bank[0][rows, 0:D], T.attn[:, S * j:S * j + S], T.wo[:, layer, j, :],
                                    start=(j == 0), stop=(j == 3))
                ins.then_inc(out_ready, 1)

            for t in range(KT):
                for late in (False, True):
                    prepare_next(0, 0, 0, t, late)

            def step(i, par, first, last):
                b = 2 * i + par
                ni, npar = after(i, par)
                for t in range(KT):
                    scores(b, i, par, t)
                    if t > 0:
                        shift(b, par, t)
                        if not last:
                            prepare_next(b + 1, ni, npar, t, False)
                        weigh_tile(b, par, t - 1)
                    else:
                        if not first:
                            weigh_tile(b - 1, 1 - par, KT - 1)
                            weigh_masked(b - 1, 1 - par)
                        pe.wait_ge(max_taken, 3 * HP * (b + 1))
                        if not last:
                            prepare_next(b + 1, ni, npar, t, False)
                        shift(b, par, t)
                        if not first:
                            denominators(b - 1)
                    if t == 2 and not first:
                        if not last:
                            pe.wait_ge(ctxT_copied, 3 * (b + 1) + 3)
                        else:
                            pe.wait_ge(recip_ready, b)
                        project(b - 1, *((i, 0) if par else (i - 1, 1)))
                    if not last:
                        prepare_next(b + 1, ni, npar, t, True)
                if last:
                    weigh_tile(b, par, KT - 1)
                    weigh_masked(b, par)
                    pe.wait_ge(x_added, b)
                    denominators(b)
                    pe.wait_ge(recip_ready, b + 1)
                    project(b, i, par)

            steps(pe, step)

        @block.scalar
        def _(act):
            def copy_turned(n, j, src):
                if j == 0:
                    above_zero(act, v_ready, 3 * n)
                act.wait_ge(ctxT_ready, 3 * n + j + 1)
                act.activation(T.ctxT[:, CHUNK * j:CHUNK * j + CHUNK], bank[src][:, 0:CHUNK], ACT.Copy)\
                   .then_inc(ctxT_copied, 1)

            def copy_keys(n, par, j, src):
                act.wait_ge(k_ready, 3 * n + j + 1)
                above_zero(act, split, 3 * n)
                act.activation(T.kf[:, CHUNK * j:CHUNK * j + CHUNK], bank[src][:, 0:CHUNK], ACT.Identity,
                               bias=T.bk[:, layer:layer + 1])
                above_zero(act, first_ready, 3 * HP * n)
                above_zero(act, stacked, STACKED * n)
                act.activation(T.kpart[0][:, CHUNK * j:CHUNK * j + CHUNK], bank[src][:, 0:CHUNK], ACT.Identity,
                               bias=T.bk[:, layer:layer + 1]).then_inc(k_copied, 1)

            def prepare_next(n, par, t):
                if t == 0:
                    copy_turned(n, 0, 1)
                    copy_turned(n, 1, 2)
                if t == 1:
                    copy_turned(n, 2, 0)
                    copy_keys(n, par, 0, 1)
                    copy_keys(n, par, 1, 2)
                if t == 2:
                    copy_keys(n, par, 2, 1)
                if t == KT - 1:
                    act.wait_ge(earg_ready, n + 1)
                    above_zero(act, de_ready, 2 * n)
                    act.activation(T.emask[:, :], T.earg[:, :], ACT.Exp).then_inc(emask_ready, 1)

            for t in range(KT):
                prepare_next(0, 0, t)

            def copy_sums(b):
                act.wait_ge(sums_ready, b + 1)
                above_zero(act, attn_ready, b)
                act.activation(T.sums[:, :], sums_ps, ACT.Copy).then_inc(sums_copied, 1)

            def step(i, par, first, last):
                b = 2 * i + par
                for t in range(KT):
                    m = KT * b + t
                    if t == 0 and not first:
                        copy_sums(b - 1)
                    act.wait_ge(scores_ready, m + 1)
                    above_zero(act, probs_used, m - 2)
                    act.activation(T.probs[t % 3][0:KP, :].rearrange("k (a c) -> k a c", a=2),
                                   scores_ps[t % 2][0:KP], ACT.Exp).then_inc(probs_ready, 1)
                    if not last:
                        prepare_next(b + 1, 1 - par, t)
                if last:
                    copy_sums(b)

            steps(act, step)

        @block.vector
        def _(dve):
            def prepare_next(n, par):
                v4 = T.v[par][:, :, 0:H * VW].rearrange("k t (h d) -> k t h d", d=VW)
                for j, src in ((0, 2), (1, 0), (2, 1)):
                    dve.wait_ge(v_ready, 3 * n + j + 1)
                    dve.tensor_tensor(v4[0:KP, 4 * j:4 * j + 4, :, 0:DH],
                                      bank[src][0:KP, :].rearrange("k (t h d) -> k t h d", t=4, h=H),
                                      T.bv[0:KP, layer, :].rearrange("k (h d) -> k h d", d=DH).unsqueeze(1)
                                      .to_broadcast([KP, 4, H, DH]), ALU.add).then_inc(v_copied, 1)
                dve.wait_ge(g_ready, n + 1)
                dve.tensor_copy(T.gt[:, 0:S], bank[2][:, 0:S])
                dve.tensor_copy(T.gt[:, HALF:HALF + S], bank[2][:, 0:S]).then_inc(g_copied, 1)
                dve.wait_ge(mv_ready, n + 1)
                dve.tensor_tensor(T.mv9[par][:, 0:H * VW].rearrange("q (h d) -> q h d", d=VW)[:, :, 0:DH],
                                  bank[0][:, 0:D].rearrange("q (h d) -> q h d", d=DH),
                                  T.countbv[:, layer, :].rearrange("q (h d) -> q h d", d=DH), ALU.add)\
                   .then_inc(mv_copied, 1)
                dve.wait_ge(qs_up, n + 1)
                above_zero(dve, qs_ready, 2 * n)
                up = bank[1][:, 0:NG * S]
                dve.tensor_copy(T.qa_rows[:, :], up).then_inc(qs_parts, 1)
                dve.wait_ge(qs_parts, 4 * n + 1)
                dve.tensor_tensor(T.qleft[:, :], up, T.qa_rows[:, :], ALU.subtract).then_inc(qs_taken, 1)
                dve.wait_ge(qs_taken, n + 1)
                dve.tensor_copy(T.qa_rows[96:P, :], T.qleft[96:P, :])
                dve.tensor_copy(T.qb_rows[0:64, :], T.qleft[0:64, :]).then_inc(qs_parts, 1)
                dve.wait_ge(qs_parts, 4 * n + 2)
                dve.tensor_tensor(T.qleft[0:GR, :], T.qleft[0:GR, :], T.qb_rows[0:GR, :], ALU.subtract)\
                   .then_inc(qs_parts, 1)
                dve.wait_ge(qs_parts, 4 * n + 3)
                dve.tensor_copy(T.qb_rows[0:GR, :], T.qleft[0:GR, :]).then_inc(qs_parts, 1)
                for p in range(HP):
                    for j in range(3):
                        keys = slice(CHUNK * j, CHUNK * j + CHUNK)
                        wait_apart(dve, T, first_ready, 3 * (HP * n + p) + j + 1, j)
                        dve.tensor_tensor_reduce(out=T.junk[:, keys], in0=bank[j][:, 0:CHUNK],
                                                 in1=T.hide[:, layer, keys],
                                                 scale=1.0, scalar=NONE, op0=ALU.add, op1=ALU.max,
                                                 accum_out=T.bankmax[:, p, j:j + 1]).then_inc(max_taken, 1)
                dve.wait_ge(max_taken, 3 * HP * (n + 1))
                dve.tensor_reduce(T.rowmax[:, :], T.bankmax[:, :, :], AX.X, ALU.max).then_inc(max_joined, 1)
                dve.wait_ge(max_joined, n + 1)
                above_zero(dve, de_ready, 2 * n)
                dve.tensor_scalar(T.negm[:, :], T.rowmax[:, :], T.floor[:, layer:layer + 1], -1.0,
                                  ALU.max, ALU.mult).then_inc(negm_ready, 1)
                dve.wait_ge(negm_ready, n + 1)
                dve.tensor_scalar(T.earg[:, :], T.negm[:, :], T.masked[layer], 0.0, ALU.add, ALU.min)\
                   .then_inc(earg_ready, 1)
                for a in range(2):
                    rows = slice(HALF * a, HALF * a + S)
                    dve.tensor_tensor(T.mvr[par][rows, a, :, :],
                                       T.idq[rows, :].unsqueeze(1).to_broadcast([S, HP, S]),
                                       T.negm[rows, :].unsqueeze(2).to_broadcast([S, HP, S]), ALU.mult)\
                        .then_inc(shift_ready, 1)
                above_zero(dve, sums_ready, n - 1)
                dve.wait_ge(emask_ready, n + 1)
                for a in range(2):
                    rows = slice(HALF * a, HALF * a + S)
                    dve.tensor_tensor(T.de[par][rows, HP * a:HP * a + HP, :],
                                       T.idq[rows, :].unsqueeze(1).to_broadcast([S, HP, S]),
                                       T.emask[rows, :].unsqueeze(2).to_broadcast([S, HP, S]), ALU.mult)\
                        .then_inc(de_ready, 1)

            def divide(b):
                dve.wait_ge(den_ready, b + 1)
                dve.reciprocal(T.recip[:, :], bank[0][:, 0:4 * S]).then_inc(recip_ready, 1)
                dve.wait_ge(recip_ready, b + 1)
                dve.tensor_tensor(T.attn[:, :], T.sums[:, :], T.recip[:, :], ALU.mult).then_inc(attn_ready, 1)

            def add_to_x(b, i, par):
                rows = slice(HALF * par, HALF * par + S)
                dve.wait_ge(out_ready, b + 1)
                dve.tensor_tensor(T.x[rows, i, :], T.x[rows, i, :], bank[0][rows, 0:D], ALU.add)\
                   .then_inc(x_added, 1)

            for par in range(2):
                dve.tensor_copy(T.mv9[par][:, 0:H * VW].rearrange("q (h d) -> q h d", d=VW)[:, :, DH:VW],
                                T.count[:, layer:layer + 1].unsqueeze(1).to_broadcast([P, H, 1]))
            prepare_next(0, 0)

            def step(i, par, first, last):
                b = 2 * i + par
                if not first:
                    divide(b - 1)
                    add_to_x(b - 1, *((i, 0) if par else (i - 1, 1)))
                if not last:
                    prepare_next(b + 1, 1 - par)
                else:
                    divide(b)
                    add_to_x(b, i, par)

            steps(dve, step)

        @block.gpsimd
        def _(pool):
            def prepare_next(n, i, par):
                above_zero(pool, first_ready, 3 * HP * n)
                above_zero(pool, scores_ready, KT * (n - 1))
                pool.tensor_tensor(T.turn[:, :], T.turn[:, :], T.turn[:, :], ALU.mult)
                q = T.qT[:, i, HALF * par:HALF * par + S]
                for a in range(2):
                    ins = pool.tensor_tensor(T.qbf[:, :, a, 0:S], q.unsqueeze(1).to_broadcast([P, HP, S]),
                                             T.headmask[:, HP * a:HP * a + HP].unsqueeze(2).to_broadcast([P, HP, S]),
                                             ALU.mult)
                ins.then_inc(q_ready, 1)
                for j in range(3):
                    cols = slice(CHUNK * j, CHUNK * j + CHUNK)
                    pool.wait_ge(k_copied, 3 * n + j + 1)
                    above_zero(pool, stacked, STACKED * n)
                    pool.tensor_tensor(T.kpart[1][:, cols], T.kf[:, cols], T.kpart[0][:, cols], ALU.subtract)\
                        .then_inc(step_split, 1)
                    pool.wait_ge(step_split, 6 * n + 2 * j + 1)
                    pool.tensor_tensor(T.kf[:, cols], T.kf[:, cols], T.kpart[0][:, cols], ALU.subtract)\
                        .then_inc(step_split, 1)
                    pool.wait_ge(step_split, 6 * n + 2 * j + 2)
                    pool.tensor_tensor(T.kpart[2][:, cols], T.kf[:, cols], T.kpart[1][:, cols], ALU.subtract)\
                        .then_inc(split, 1)
                pool.wait_ge(qs_parts, 4 * n + 4)
                for dst, rows, top in ((T.qa[par], T.qa_rows, P), (T.qb[par], T.qb_rows, 2 * GR)):
                    pool.tensor_tensor(dst[0:top, :, :, :],
                                       rows[0:top, :].rearrange("r (g q) -> r g q", q=S).unsqueeze(2)
                                       .to_broadcast([top, NG, 4, S]),
                                       T.groupmask[0:top, :].unsqueeze(1).unsqueeze(3)
                                       .to_broadcast([top, NG, 4, S]), ALU.mult).then_inc(qs_ready, 1)

            prepare_next(0, 0, 0)

            def step(i, par, first, last):
                if not last:
                    prepare_next(2 * i + par + 1, *after(i, par))

            steps(pool, step)


def part_gates(eng, T, step, count):
    gates = T.psum[:, 4:8, :].rearrange("p b n -> p (b n)")
    for rows, left in ((3 * E0, gates), (2 * E0, T.gate_left), (E0, T.gate_left)):
        eng.tensor_copy(T.gate_parts[0:rows, :], left[0:rows, :]).then_inc(step, 1)
        count += 1
        eng.wait_ge(step, count)
        if rows > E0:
            eng.tensor_tensor(T.gate_left[0:rows - E0, :], left[0:rows - E0, :], T.gate_parts[0:rows - E0, :],
                              ALU.subtract).then_inc(step, 1)
            count += 1
            eng.wait_ge(step, count)


def gates0(nc, ctx, T):
    sem = lambda n: ctx.enter_context(nc.semaphore(f"g0_{n}"))
    logits, scored, step, chosen, counted, gated, turned = (
        sem("logits"), sem("scored"), sem("step"), sem("chosen"), sem("counted"), sem("gated"), sem("turned"))
    top_done, idx_done = sem("top"), sem("idx")
    flat = lambda t: t.rearrange("p i e -> p (i e)")
    with nc.Block() as block:

        @block.tensor
        def _(pe):
            for i in range(NS):
                ins = pe.matmul(T.psum[:, 0, E0 * i:E0 * i + E0], T.xT[:, i, :], T.gw[:, :], start=True, stop=True)
            ins.then_inc(logits, 1)
            pe.wait_ge(chosen, 1)
            pe.matmul(T.psum[:, 1, :], T.earlier[:, :], flat(T.sel_b[:, :, :]), start=True, stop=True)
            pe.matmul(T.psum[:, 2, :], T.ones_b[:, :], flat(T.sel_b[:, :, :]), start=True, stop=True)\
              .then_inc(counted, 1)
            pe.wait_ge(gated, 1)
            for i in range(NS):
                ins = pe.transpose(T.psum[0:3 * E0, 4 + i // 4, P * (i % 4):P * (i % 4) + P], T.gate3[:, i, :],
                                   T.ident[:, :])
            ins.then_inc(turned, 1)

        @block.scalar
        def _(act):
            act.wait_ge(logits, 1)
            act.activation(flat(T.score[:, :, :]), T.psum[:, 0, :], ACT.Sigmoid).then_inc(scored, 1)

        @block.vector
        def _(dve):
            n = [0]

            def after(ins):
                ins.then_inc(step, 1)
                n[0] += 1
                dve.wait_ge(step, n[0])

            dve.wait_ge(scored, 1)
            after(dve.tensor_tensor(T.biased[:, :, :], T.score[:, :, :],
                                    T.ebias[:, :].unsqueeze(1).to_broadcast([P, NS, E0]), ALU.add))
            for i in range(NS):
                dve.max(T.top[:, i, :], T.biased[:, i, :]).then_inc(top_done, 1)
                dve.wait_ge(top_done, i + 1)
                dve.max_index(T.idx[:, i, :], T.top[:, i, :], T.biased[:, i, :]).then_inc(idx_done, 1)
            dve.wait_ge(idx_done, NS)
            after(dve.tensor_copy(T.idx_f[:, :, :], T.idx[:, :, :]))
            for k in range(TOPK):
                dst = T.sel if k == 0 else T.hot
                after(dve.tensor_tensor(dst[:, :, :], T.iota_f[:, :].unsqueeze(1).to_broadcast([P, NS, E0]),
                                        T.idx_f[:, :, k:k + 1].to_broadcast([P, NS, E0]), ALU.is_equal))
                if k:
                    after(dve.tensor_tensor(T.sel[:, :, :], T.sel[:, :, :], T.hot[:, :, :], ALU.add))
            dve.tensor_scalar(T.sel_b[:, :, :], T.sel[:, :, :], T.rowvalid[:, 0:1], None, ALU.mult)\
               .then_inc(chosen, 1)
            after(dve.tensor_tensor(T.gate[:, :, :], T.score[:, :, :], T.sel[:, :, :], ALU.mult))
            after(dve.tensor_reduce(T.wsum[:, :], T.gate[:, :, :], AX.X, ALU.add))
            after(dve.tensor_scalar(T.wsum[:, :], T.wsum[:, :], 1e-12, None, ALU.max))
            after(dve.reciprocal(T.wsum[:, :], T.wsum[:, :]))
            after(dve.tensor_tensor(T.gate[:, :, :], T.gate[:, :, :],
                                    T.wsum[:, :].unsqueeze(2).to_broadcast([P, NS, E0]), ALU.mult))
            dve.wait_ge(counted, 1)
            after(dve.memset(T.before[:, 0, :], 0.0))
            for i in range(1, NS):
                after(dve.tensor_tensor(T.before[:, i, :], T.before[:, i - 1, :],
                                        T.psum[:, 2, E0 * (i - 1):E0 * i], ALU.add))
            after(dve.tensor_tensor(flat(T.before[:, :, :]), flat(T.before[:, :, :]), T.psum[:, 1, :], ALU.add))
            after(dve.tensor_scalar(T.before[:, :, :], T.before[:, :, :], float(CAP), None, ALU.is_lt))
            gate3 = T.gate3[:, :, :].rearrange("p i (r e) -> p i r e", e=E0)
            for r in range(3):
                ins = dve.tensor_tensor(gate3[:, :, r, :], T.gate[:, :, :], T.before[:, :, :], ALU.mult)
            ins.then_inc(gated, 1)
            dve.wait_ge(turned, 1)
            part_gates(dve, T, step, n[0])


def gates1(nc, ctx, T):
    sem = lambda n: ctx.enter_context(nc.semaphore(f"g1_{n}"))
    logits, shifted, expd, step, gated, turned = (
        sem("logits"), sem("shifted"), sem("expd"), sem("step"), sem("gated"), sem("turned"))
    top_done, idx_done = sem("top"), sem("idx")
    lg = T.score[:, :, 0:E1]
    with nc.Block() as block:

        @block.tensor
        def _(pe):
            for i in range(NS):
                ins = pe.matmul(T.psum[:, 0, E1 * i:E1 * i + E1], T.xT[:, i, :], T.wr[:, :], start=True, stop=True)
            ins.then_inc(logits, 1)
            pe.wait_ge(gated, 1)
            for i in range(NS):
                ins = pe.transpose(T.psum[0:3 * E0, 4 + i // 4, P * (i % 4):P * (i % 4) + P], T.gate3[:, i, :],
                                   T.ident[:, :])
            ins.then_inc(turned, 1)

        @block.scalar
        def _(act):
            act.wait_ge(shifted, 1)
            act.activation(T.biased[:, :, 0:E1], lg, ACT.Exp).then_inc(expd, 1)

        @block.vector
        def _(dve):
            n = [0]

            def after(ins):
                ins.then_inc(step, 1)
                n[0] += 1
                dve.wait_ge(step, n[0])

            dve.wait_ge(logits, 1)
            after(dve.tensor_tensor(lg, T.psum[:, 0, 0:NS * E1].rearrange("p (i e) -> p i e", e=E1),
                                    T.br[:, :].unsqueeze(1).to_broadcast([P, NS, E1]), ALU.add))
            after(dve.tensor_reduce(T.wsum[:, :], lg, AX.X, ALU.max))
            dve.tensor_tensor(lg, lg, T.wsum[:, :].unsqueeze(2).to_broadcast([P, NS, E1]), ALU.subtract)\
               .then_inc(shifted, 1)
            dve.wait_ge(expd, 1)
            for i in range(NS):
                dve.max(T.top[:, i, :], T.biased[:, i, 0:E1]).then_inc(top_done, 1)
                dve.wait_ge(top_done, i + 1)
                dve.max_index(T.idx[:, i, :], T.top[:, i, :], T.biased[:, i, 0:E1]).then_inc(idx_done, 1)
            dve.wait_ge(idx_done, NS)
            after(dve.tensor_copy(T.idx_f[:, :, :], T.idx[:, :, :]))
            after(dve.tensor_reduce(T.wsum[:, :], T.biased[:, :, 0:E1], AX.X, ALU.add))
            after(dve.reciprocal(T.wsum[:, :], T.wsum[:, :]))
            after(dve.tensor_tensor(T.wsum[:, :], T.wsum[:, :], T.top[:, :, 0], ALU.mult))
            after(dve.tensor_tensor(T.hot[:, :, 0:E1], T.iota_f[:, 0:E1].unsqueeze(1).to_broadcast([P, NS, E1]),
                                    T.idx_f[:, :, 0:1].to_broadcast([P, NS, E1]), ALU.is_equal))
            dve.tensor_tensor(T.gate[:, :, 0:E1], T.hot[:, :, 0:E1],
                              T.wsum[:, :].unsqueeze(2).to_broadcast([P, NS, E1]), ALU.mult).then_inc(step, 1)
            n[0] += 1
            dve.wait_ge(step, n[0])
            after(dve.memset(T.gate3[:, :, :], 0.0))
            gate3 = T.gate3[:, :, :].rearrange("p i (r e) -> p i r e", e=E0)
            for r in range(3):
                ins = dve.tensor_copy(gate3[:, :, r, 0:E1], T.gate[:, :, 0:E1])
            ins.then_inc(gated, 1)
            dve.wait_ge(turned, 1)
            dve.tensor_copy(T.gateT[:, :], T.psum[0:E1, 4:8, :].rearrange("p b n -> p (b n)"))
            part_gates(dve, T, step, n[0])


def experts(nc, ctx, T, layer):
    sem = lambda n: ctx.enter_context(nc.semaphore(f"e{layer}_{n}"))
    staged, up_ready, side_ready, gate_ready = sem("staged"), sem("up_ready"), sem("side_ready"), sem("gate_ready")
    act_done, prod_done, gated, down_done = sem("act_done"), sem("prod_done"), sem("gated"), sem("down_done")
    y_copied, y_turned = sem("y_copied"), sem("y_turned")
    units = 17 if layer == 0 else 16
    per = 3 if layer == 0 else 2
    chunk = lambda t, c, rows=P: t[0:rows, 4 * c:4 * c + 4, :].rearrange("p i (b q) -> p (i b) q", b=2)[:, :, 0:S]
    gateT = T.gateT[:, :].rearrange("p (i q) -> p i q", q=P)
    parts = T.gate_parts[:, :].rearrange("p (i q) -> p i q", q=P)
    N = 8 * S
    W1, W3, W2, PK = T.stage

    def run(eng, unit):
        unit(0, 0)
        with eng.Fori(0, 7) as k:
            unit(2 * k + 1, 1)
            unit(2 * k + 2, 0)
        for u in range(15, units):
            unit(u, u % 2)

    with nc.Block() as block:

        @block.tensor
        def _(pe):
            def down(u, par, c, first, last):
                m = 4 * u + c
                pe.wait_ge(gated, m + 1)
                pe.matmul(T.psum[:, c, 0:N], W2[par][:, :], T.hid[c % 2][:, :], start=first,
                          stop=last, skip_group_check=True).then_inc(down_done, 1)

            def unit(u, par, first, with_prev):
                pe.wait_ge(staged, u + 1)
                for c in range(TOKC):
                    m = 4 * u + c
                    hb = [T.psum[:, 4 + (per * c + k) % 4, 0:N] for k in range(per)]
                    if layer == 0:
                        above_zero(pe, gated, m - 1)
                        pe.matmul(hb[0], W1[par][:, :], chunk(T.xT, c), start=True, stop=True).then_inc(up_ready, 1)
                        above_zero(pe, act_done, m)
                        pe.matmul(hb[1], W3[par][:, :], chunk(T.xT, c), start=True, stop=True).then_inc(side_ready, 1)
                        if isinstance(u, int) and u == 16:
                            if c > 0:
                                down(u, par, c - 1, first, False)
                            elif with_prev:
                                down(u - 1, 1 - par, 3, False, False)
                            continue
                        above_zero(pe, prod_done, m)
                        if not (isinstance(u, int) and u == 16):
                            pe.matmul(hb[2], PK[par][0:3 * E0, :], chunk(parts, c, 3 * E0), start=True, stop=True)\
                              .then_inc(gate_ready, 1)
                    else:
                        above_zero(pe, act_done, m - 1)
                        pe.matmul(hb[0], W1[par][:, :], chunk(T.xT, c), start=True, stop=True).then_inc(up_ready, 1)
                        above_zero(pe, gated, m - 1)
                        pe.matmul(hb[1], PK[par][0:3 * E0, :], chunk(parts, c, 3 * E0), start=True, stop=True)\
                          .then_inc(gate_ready, 1)
                    if c > 0:
                        down(u, par, c - 1, first, False)
                    elif with_prev:
                        down(u - 1, 1 - par, 3, False, False)

            unit(0, 0, True, False)
            down(0, 0, 3, True, False)
            with pe.Fori(0, 7) as k:
                unit(2 * k + 1, 1, False, False)
                unit(2 * k + 2, 0, False, True)
                down(2 * k + 2, 0, 3, False, False)
            for u in range(15, units):
                unit(u, u % 2, False, u > 15)
            down(units - 1, (units - 1) % 2, 3, False, True)
            if layer == 1:
                for c in range(TOKC):
                    ins = pe.matmul(T.psum[:, c, 0:N], T.b2[0:E1, :], chunk(gateT, c, E1), start=False,
                                    stop=True, skip_group_check=True)
                ins.then_inc(down_done, 1)
            pe.wait_ge(y_copied, TOKC)
            for i in range(NS):
                ins = pe.transpose(T.psum[:, 4 + i // 4, P * (i % 4):P * (i % 4) + P], T.xT[:, i, :], T.ident[:, :])
            ins.then_inc(y_turned, 1)

        @block.scalar
        def _(act):
            def unit(u, par):
                for c in range(TOKC):
                    m = 4 * u + c
                    act.wait_ge(up_ready, m + 1)
                    above_zero(act, prod_done if layer == 0 and not (isinstance(u, int) and u == 16 and c > 1)
                               else gated, m - 1)
                    src = T.psum[:, 4 + (per * c) % 4, 0:N]
                    if layer == 0:
                        act.activation(T.acted[c % 2][:, :], src, ACT.Silu).then_inc(act_done, 1)
                    else:
                        act.activation(T.acted[c % 2][:, :], src, ACT.Gelu, bias=T.b1_now[par][:, :]).then_inc(act_done, 1)

            run(act, unit)
            act.wait_ge(down_done, 4 * units + layer)
            for c in range(TOKC):
                act.activation(chunk(T.xT, c), T.psum[:, c, 0:N].rearrange("p (i q) -> p i q", q=S), ACT.Copy)\
                   .then_inc(y_copied, 1)

        @block.vector
        def _(dve):
            def stage(u, par):
                copies = [(W1, T.w1[layer]), (W2, T.w2[layer])]
                if not (isinstance(u, int) and u == 16):
                    copies.insert(0, (PK, T.pick[layer]))
                if layer == 0:
                    copies.insert(0, (W3, T.w3))
                else:
                    copies.insert(0, (T.b1_now, T.b1))
                above_zero(dve, down_done, 4 * (u - 1))
                for dst, src in copies:
                    ins = dve.tensor_scalar(dst[par][:, :], src[:, u, :], 1.0, None, ALU.mult)
                ins.then_inc(staged, 1)

            stage(0, 0)

            def unit(u, par):
                for c in range(TOKC):
                    m = 4 * u + c
                    if c == 2 and not (isinstance(u, int) and u == units - 1):
                        stage(u + 1, 1 - par)
                    dve.wait_ge(act_done, m + 1)
                    if layer == 0:
                        dve.wait_ge(side_ready, m + 1)
                        above_zero(dve, gated, m - 1)
                        if isinstance(u, int) and u == 16:
                            above_zero(dve, down_done, m - 1)
                            dve.tensor_tensor(T.hid[c % 2][:, :], T.acted[c % 2][:, :],
                                              T.psum[:, 4 + (per * c + 1) % 4, 0:N], ALU.mult).then_inc(gated, 1)
                            continue
                        dve.tensor_tensor(T.prod[c % 2][:, :], T.acted[c % 2][:, :], T.psum[:, 4 + (per * c + 1) % 4, 0:N],
                                          ALU.mult).then_inc(prod_done, 1)
                        dve.wait_ge(prod_done, m + 1)
                    dve.wait_ge(gate_ready, m + 1)
                    above_zero(dve, down_done, m - 1)
                    dve.tensor_tensor(T.hid[c % 2][:, :], T.prod[c % 2][:, :] if layer == 0 else T.acted[c % 2][:, :],
                                      T.psum[:, 4 + (per * c + per - 1) % 4, 0:N], ALU.mult).then_inc(gated, 1)

            run(dve, unit)
            dve.wait_ge(y_turned, 1)
            for b in range(4):
                dve.tensor_tensor(T.x[:, 4 * b:4 * b + 4, :], T.x[:, 4 * b:4 * b + 4, :],
                                  T.psum[:, 4 + b, :].rearrange("p (i d) -> p i d", d=D), ALU.add)


def cross_attention_ffn_kernel(nc, A, out):
    with ExitStack() as ctx:
        def sb(name, shape, dt=F32):
            return ctx.enter_context(nc.sbuf_tensor(name, shape, dt))

        T = Tiles()
        T.psum = ctx.enter_context(nc.psum_tensor("psum", [P, 8, 512], F32))
        T.masked = [-173.0 * 2.0 ** 59, 1e-9]
        T.x = sb("x_rows", [P, NS, D])
        T.xn = sb("xn", [P, NS, D])
        T.xT = sb("xT", [P, NS, P])
        T.qT = T.xn
        T.w_t = sb("w_t", [P, 2, 3, D])
        T.bq, T.bk = sb("bq", [P, 2]), sb("bk", [P, 2])
        T.bv, T.bo = sb("bv", [P, 2, D]), sb("bo", [P, 2, D])
        T.wo = sb("wo", [P, 2, 4, D])
        T.gw_in, T.gw = sb("gw_in", [E0, D], BF16), sb("gw", [P, E0])
        T.sw1_in, T.sw3_in = sb("sw1_in", [I0, D], BF16), sb("sw3_in", [I0, D], BF16)
        T.sw2_in = sb("sw2_in", [D, I0], BF16)
        T.ebias, T.wr, T.br = sb("ebias", [P, E0]), sb("wr", [P, E1]), sb("br", [P, E1])
        T.b1, T.b2 = sb("b1", [P, 16, 1]), sb("b2", [E1, D])
        T.w1 = [sb("w1_0", [P, 17, P], BF16)]
        T.w3 = sb("w3", [P, 17, P], BF16)
        T.w2 = [sb("w2_0", [P, 17, D], BF16)]
        T.pick = [sb("pick_0", [P, 16, P], BF16), sb("pick_1", [P, 16, P], BF16)]
        T.b1_now = [sb(f"b1_now{k}", [P, 1]) for k in range(2)]
        T.ident, T.ident_b = sb("ident", [P, P]), sb("ident_b", [P, P], BF16)
        T.headmask, T.densel = sb("headmask", [P, H]), sb("densel", [P, 4, P])
        T.earlier, T.ones_b = sb("earlier", [P, P], BF16), sb("ones_b", [P, P], BF16)
        T.iota_i, T.iota_f, T.rowvalid = sb("iota_i", [P, E0], I32), sb("iota_f", [P, E0]), sb("rowvalid", [P, 1])
        T.idq = sb("idq", [P, S])
        T.hide = sb("hide", [P, 2, SK], BF16)
        T.mkT = sb("mkT", [P, 2, KT, S])
        T.shiftw = sb("shiftw", [P, 2, 2, SK], BF16)
        T.count, T.floor, T.tmp1 = sb("count", [P, 2]), sb("floor", [P, 2]), sb("tmp1", [P, 1])
        T.countbv = sb("countbv", [P, 2, D])
        T.stats, T.moments = sb("stats", [P, NS, 6]), sb("moments", [P, NS, 2])
        T.var, T.std, T.rstd = sb("var", [P, NS]), sb("std", [P, NS]), sb("rstd", [P, NS, 1])
        T.ctx = [sb(f"ctx{k}", [P, KT, D]) for k in range(2)]
        T.mask0 = T.ctx[0][:].rearrange("p t d -> p (t d)")[:, 0:SK].bitcast(I32)
        T.mask1 = T.ctx[1][:].rearrange("p t d -> p (t d)")[:, 0:SK // 4].bitcast(I32)
        T.ctxT = sb("ctxT", [P, SK])
        T.kf = sb("k_full", [P, SK])
        T.ks = sb("k_stacked", [P, 2, NG, SK], BF16)
        T.stackq, T.groupmask = sb("stackq", [P, NG, P]), sb("groupmask", [P, NG])
        T.qa_rows, T.qb_rows = sb("qa_rows", [P, NG * S], BF16), sb("qb_rows", [P, NG * S], BF16)
        T.qleft = sb("q_left", [P, NG * S])
        T.mk = T.kf[:, :].bitcast(BF16).rearrange("p (l k) -> p l k", l=2)
        T.kpart = [sb(f"k_part{k}", [P, SK], BF16) for k in range(3)]
        T.v = [sb(f"v{k}", [P, KT, VCOLS]) for k in range(2)]
        T.probs = [sb(f"probs{k}", [P, H * S]) for k in range(3)]
        T.w_in = T.probs[0][:, 0:6 * D].rearrange("p (l k n) -> p l k n", l=2, k=3)
        T.woa = T.probs[1][:, 0:4 * D].rearrange("p (j n) -> p j n", j=4)
        T.wo_in = T.probs[2][:, 0:D]
        T.qa = [sb(f"q_stacked_a{k}", [P, NG, 4, S], BF16) for k in range(2)]
        T.qb = [sb(f"q_stacked_b{k}", [P, NG, 4, S], BF16) for k in range(2)]
        T.qbf = sb("qbf", [P, HP, 2, HALF], BF16)
        T.mvr = [sb(f"shift_rows{k}", [P, 2, HP, S], BF16) for k in range(2)]
        T.de = [sb(f"masked_weights{k}", [P, H, S]) for k in range(2)]
        T.mv9 = [sb(f"masked_values{k}", [P, VCOLS]) for k in range(2)]
        T.gt = sb("masked_ctx", [P, P])
        T.junk = sb("junk", [P, SK], BF16)
        T.bankmax = sb("bankmax", [P, HP, 3])
        T.rowmax, T.negm, T.emask = sb("rowmax", [P, HP]), sb("negm", [P, HP], BF16), sb("emask", [P, HP])
        T.earg = sb("earg", [P, HP])
        T.sums, T.recip, T.attn = sb("sums", [P, 4 * S]), sb("recip", [P, 4 * S]), sb("attn", [P, 4 * S])
        T.gateT = sb("gateT", [E1, NS * P])
        ks = T.ks[:, :, :, :].rearrange("p b g k -> p (b g k)").bitcast(F32)
        T.w1.append(ks[:, 0:16 * P].rearrange("p (u f) -> p u f", f=P))
        T.w2.append(ks[:, 16 * P:32 * P].rearrange("p (u f) -> p u f", f=P))
        T.stage = [[ks[:, (32 + 2 * n + k) * P:(33 + 2 * n + k) * P] for k in range(2)] for n in range(4)]
        T.stage[3] = [tile.bitcast(BF16)[:, 0:P] for tile in T.stage[3]]
        flat_k = [T.kf, ks[:, 40 * P:40 * P + 864]]
        T.sel = T.probs[0][:, 0:512].rearrange("p (i e) -> p i e", e=E0)
        T.hot = T.probs[1][:, 0:512].rearrange("p (i e) -> p i e", e=E0)
        T.gate = T.probs[2][:, 0:512].rearrange("p (i e) -> p i e", e=E0)
        T.score = flat_k[0][:, 0:512].rearrange("p (i e) -> p i e", e=E0)
        T.biased = flat_k[0][:, 512:1024].rearrange("p (i e) -> p i e", e=E0)
        T.before = flat_k[1][:, 0:512].rearrange("p (i e) -> p i e", e=E0)
        T.gate3 = T.ctx[0][:, :, :].rearrange("p t d -> p (t d)").rearrange("p (i e) -> p i e", e=3 * E0)
        T.gate_parts = T.ctx[1][:, :, :].rearrange("p t d -> p (t d)").bitcast(BF16)[:, 0:NS * P]
        T.gate_left = T.xn[:, :, :].rearrange("p i d -> p (i d)")
        T.sel_b = T.qa[0][:, :, :, :].rearrange("p g h q -> p (g h q)")[:, 0:512].rearrange("p (i e) -> p i e", e=E0)
        T.top = T.sums[:, 0:NS * 8].rearrange("p (i e) -> p i e", e=8)
        T.idx = T.recip[:, 0:NS * 8].bitcast(U32).rearrange("p (i e) -> p i e", e=8)
        T.idx_f = T.attn[:, 0:NS * 8].rearrange("p (i e) -> p i e", e=8)
        T.wsum = sb("wsum", [P, NS])
        N = 8 * S
        T.acted = [T.ctxT[:, N * k:N * k + N] for k in range(2)]
        T.prod = [T.ctxT[:, 2 * N:3 * N], flat_k[0][:, 0:N]]
        T.hid = [T.kf[:, 512:512 + N], T.kf[:, 512 + N:512 + 2 * N]]
        T.carrier, T.turn = sb("carrier", [P, 3]), sb("turn", [P, 1])

        constants_and_loads(nc, ctx, A, T)
        prepare(nc, ctx, A, T)
        normalise(nc, ctx, T, "n0")
        queries(nc, ctx, T, 0)
        attention(nc, ctx, A, T, 0)
        normalise(nc, ctx, T, "n1")
        gates0(nc, ctx, T)
        experts(nc, ctx, T, 0)
        normalise(nc, ctx, T, "n2")
        queries(nc, ctx, T, 1)
        attention(nc, ctx, A, T, 1)
        normalise(nc, ctx, T, "n3", (A["L1_ffn_W1"], A["L1_ffn_W2"]))
        gates1(nc, ctx, T)
        experts(nc, ctx, T, 1)

        stored = ctx.enter_context(nc.semaphore("stored"))
        with nc.Block() as block:

            @block.sync
            def _(sp):
                for par in range(2):
                    sp.dma_start(out.rearrange("(i two) q d -> two q i d", two=2)[par],
                                 T.x[HALF * par:HALF * par + S, :, :]).then_inc(stored, 16)
                sp.wait_ge(stored, 32)


_INS = ['x', 'ctx_1024', 'mask_1x1xSxS2_ik0', 'mask_1x1xSxS2_bk0'] + \
       [f'L{j}_xattn_{w}' for j in range(2) for w in ('Wq', 'bq', 'Wk', 'bk', 'Wv', 'bv', 'Wo', 'bo')] + \
       [f'L0_ffn_{w}' for w in ('gate_w', 'bias', 'W1', 'W3', 'W2', 'sw1', 'sw3', 'sw2')] + \
       [f'L1_ffn_{w}' for w in ('Wr', 'br', 'W1', 'b1', 'W2', 'b2')]


def kernel(**inputs):
    import numpy as _np
    import concourse.bacc as _bacc
    from concourse import mybir as _mybir
    from concourse.bass_utils import run_bass_kernel_spmd as _run

    nc = _bacc.Bacc("TRN2", target_bir_lowering=False, num_devices=1)
    arrays, aps = {}, {}
    for name in _INS:
        a = _np.ascontiguousarray(inputs[name])
        if a.dtype == _np.bool_:
            a = a.view(_np.int32)
        arrays[f"in_{name}"] = a
        aps[name] = nc.dram_tensor(f"in_{name}", a.shape, _mybir.dt.from_np(a.dtype), kind="ExternalInput").ap()
    out = nc.dram_tensor("out_x", (NB, S, D), F32, kind="ExternalOutput").ap()
    cross_attention_ffn_kernel(nc, aps, out)
    r = _run(nc, [arrays], core_ids=[0])
    return r.results[0]["out_x"]
```
